# Optimizing a Trainium2 kernel written in Bass

```python
import numpy as np
import jax
import jax.numpy as jnp

def _softmax(x, axis=-1):
    return jax.nn.softmax(x, axis=axis)

def _gelu(x):
    return jax.nn.gelu(x, approximate=True)

def _silu(x):
    return jax.nn.silu(x)

def _sigmoid(x):
    return jax.nn.sigmoid(x)

def _layernorm(x, axis=-1, eps=1e-05):
    m = jnp.mean(x, axis=axis, keepdims=True)
    v = jnp.var(x, axis=axis, keepdims=True)
    return (x - m) / jnp.sqrt(v + eps)

def _scatter_add(tgt, idx, src, axis=0):
    return tgt.at[idx].add(src)

def _segment_sum(src, seg, n):
    return jax.ops.segment_sum(src, seg, n)
kernel_name = 'mk_cond_seq_d1_seqx_r2_d9c5c8'

def setup_inputs(seed: int=0):
    np.random.seed(seed)
    _w = jnp.asarray

    def _rec_inputs():
        import jax
        import jax.numpy as jnp
        _rk = jax.random.key(seed)
        x = 7.22e-05 + 1 * jax.random.normal(jax.random.fold_in(_rk, 1), (2, 2048, 512), jnp.float32)
        _lenS = 2048 - jax.random.randint(jax.random.fold_in(_rk, 7), (2,), 0, max(1, 2048 // 4) + 1, jnp.int32)
        _lenS2 = 2048 - jax.random.randint(jax.random.fold_in(_rk, 8), (2,), 0, max(1, 2048 // 4) + 1, jnp.int32)
        cond_1024 = 0.00782532 + 1.00527 * jax.random.normal(jax.random.fold_in(_rk, 11), (2, 512), jnp.float32)
        return (x, cond_1024)
    x, cond_1024 = _rec_inputs()

    def _L0_cond_setup():
        import jax, jax.numpy as jnp
        import numpy as np
        H = 512
        NH = 16
        DH = H // NH
        MLP = 4 * H
        EPS = 1e-05

        def _ln(x):
            m = jnp.mean(x, axis=-1, keepdims=True)
            v = jnp.mean((x - m) ** 2, axis=-1, keepdims=True)
            return (x - m) * jax.lax.rsqrt(v + EPS)

        def _modulate(x, shift, scale):
            return x * (1.0 + scale[:, None, :]) + shift[:, None, :]
        key = jax.random.key(seed)
        ks = jax.random.split(key, 12)
        s = 1.0 / np.sqrt(H)
        inp = {'x': jax.random.normal(ks[0], (8, 512, H), jnp.float32), 'c': jax.random.normal(ks[1], (8, H), jnp.float32), 'Wc': jax.random.normal(ks[2], (H, 6 * H), jnp.float32) * s, 'bc': jnp.zeros((6 * H,), jnp.float32), 'Wq': jax.random.normal(ks[3], (H, H), jnp.float32) * s, 'bq': jnp.zeros((H,), jnp.float32), 'Wk': jax.random.normal(ks[4], (H, H), jnp.float32) * s, 'bk': jnp.zeros((H,), jnp.float32), 'Wv': jax.random.normal(ks[5], (H, H), jnp.float32) * s, 'bv': jnp.zeros((H,), jnp.float32), 'Wo': jax.random.normal(ks[6], (H, H), jnp.float32) * s, 'bo': jnp.zeros((H,), jnp.float32), 'W1': jax.random.normal(ks[7], (H, MLP), jnp.float32) * s, 'b1': jnp.zeros((MLP,), jnp.float32), 'W2': jax.random.normal(ks[8], (MLP, H), jnp.float32) * (1.0 / np.sqrt(MLP)), 'b2': jnp.zeros((H,), jnp.float32)}
        return inp
    _L0_cond_all = _L0_cond_setup()
    _L0_cond_in = {k: v for k, v in _L0_cond_all.items() if k in ('Wc', 'bc', 'Wq', 'bq', 'Wk', 'bk', 'Wv', 'bv', 'Wo', 'bo', 'W1', 'b1', 'W2', 'b2')}
    del _L0_cond_all
    return {'x': x, 'cond_1024': cond_1024, 'L0_cond_Wc': _L0_cond_in['Wc'], 'L0_cond_bc': _L0_cond_in['bc'], 'L0_cond_Wq': _L0_cond_in['Wq'], 'L0_cond_bq': _L0_cond_in['bq'], 'L0_cond_Wk': _L0_cond_in['Wk'], 'L0_cond_bk': _L0_cond_in['bk'], 'L0_cond_Wv': _L0_cond_in['Wv'], 'L0_cond_bv': _L0_cond_in['bv'], 'L0_cond_Wo': _L0_cond_in['Wo'], 'L0_cond_bo': _L0_cond_in['bo'], 'L0_cond_W1': _L0_cond_in['W1'], 'L0_cond_b1': _L0_cond_in['b1'], 'L0_cond_W2': _L0_cond_in['W2'], 'L0_cond_b2': _L0_cond_in['b2']}

def reference(x, cond_1024, L0_cond_Wc, L0_cond_bc, L0_cond_Wq, L0_cond_bq, L0_cond_Wk, L0_cond_bk, L0_cond_Wv, L0_cond_bv, L0_cond_Wo, L0_cond_bo, L0_cond_W1, L0_cond_b1, L0_cond_W2, L0_cond_b2):
    import jax
    import jax.numpy as jnp

    def _L0_cond_ref(x, c, Wc, bc, Wq, bq, Wk, bk, Wv, bv, Wo, bo, W1, b1, W2, b2):
        import jax, jax.numpy as jnp
        import numpy as np
        H = 512
        NH = 16
        DH = H // NH
        MLP = 4 * H
        EPS = 1e-05

        def _ln(x):
            m = jnp.mean(x, axis=-1, keepdims=True)
            v = jnp.mean((x - m) ** 2, axis=-1, keepdims=True)
            return (x - m) * jax.lax.rsqrt(v + EPS)

        def _modulate(x, shift, scale):
            return x * (1.0 + scale[:, None, :]) + shift[:, None, :]
        B, S, _ = x.shape
        c6 = jax.nn.silu(c) @ Wc + bc
        sh_msa, sc_msa, g_msa, sh_mlp, sc_mlp, g_mlp = jnp.split(c6, 6, axis=-1)
        xm = _modulate(_ln(x), sh_msa, sc_msa)
        q = (xm @ Wq + bq).reshape(B, S, NH, DH)
        k = (xm @ Wk + bk).reshape(B, S, NH, DH)
        v = (xm @ Wv + bv).reshape(B, S, NH, DH)
        q = q / DH
        w = jnp.einsum('bqhc,bkhc->bhqk', q, k)
        w = jax.nn.softmax(w, axis=-1)
        y = jnp.einsum('bhqk,bkhc->bqhc', w, v).reshape(B, S, H)
        x = x + g_msa[:, None, :] * (y @ Wo + bo)
        xm2 = _modulate(_ln(x), sh_mlp, sc_mlp)
        h = jax.nn.gelu(xm2 @ W1 + b1, approximate=False)
        x = x + g_mlp[:, None, :] * (h @ W2 + b2)
        return x
    x = _L0_cond_ref(x, cond_1024, L0_cond_Wc, L0_cond_bc, L0_cond_Wq, L0_cond_bq, L0_cond_Wk, L0_cond_bk, L0_cond_Wv, L0_cond_bv, L0_cond_Wo, L0_cond_bo, L0_cond_W1, L0_cond_b1, L0_cond_W2, L0_cond_b2)
    return x

_drawn_inputs = setup_inputs


def setup_inputs(seed=0):
    import zlib

    import numpy as np

    out = dict(_drawn_inputs(seed))
    spreads = {'L0_cond_bc': (0.0, 0.1),
     'L0_cond_bq': (0.0, 0.8),
     'L0_cond_bk': (0.0, 0.8),
     'L0_cond_bv': (0.0, 0.1),
     'L0_cond_bo': (0.0, 0.1),
     'L0_cond_b1': (0.0, 0.1),
     'L0_cond_b2': (0.0, 0.1)}
    factors = {'L0_cond_Wq': 4.643, 'L0_cond_Wk': 4.55}
    for name, (base, spread) in spreads.items():
        noise = np.random.default_rng([zlib.crc32(name.encode()), seed]).standard_normal(out[name].shape)
        drawn = base * np.exp(spread * noise) if base else spread * noise
        out[name] = jnp.asarray(drawn.astype(out[name].dtype))
    for name, factor in factors.items():
        out[name] = (out[name] * factor).astype(out[name].dtype)
    return out
```

```python
import concourse.bass as bass
from concourse import mybir
from contextlib import ExitStack

F32 = mybir.dt.float32
F32R = mybir.dt.float32r
ALU = mybir.AluOpType
ACT = mybir.ActivationFunctionType
AX = mybir.AxisListType

P = 128
B, S, H = 2, 2048, 512
NH = 16
DH = H // NH
MLP = 4 * H
EPS = 1e-5
KT = H // P
HPG = P // DH
G = NH // HPG
TOK = 512
TT = TOK // P
NBLK = B * S // TOK
BPB = S // TOK
NKT = S // P
MT = MLP // P

ROW_BC, ROW_BQ, ROW_BK, ROW_BV, ROW_B1, ROW_C = 0, 6 * KT, 7 * KT, 8 * KT, 9 * KT, 9 * KT + MT
ROWS = ROW_C + B * KT
SCALE_MSA, SHIFT_MSA, SCALE_MLP, SHIFT_MLP = 0, KT, 2 * KT, 3 * KT
G_MSA, GBO, G_MLP, GB2 = range(4)


class Shared:

    def __init__(self, nc, ctx):
        def sb(name, shape):
            return ctx.enter_context(nc.sbuf_tensor(name, shape, F32))

        self.ident = sb("ident", [P, P])
        self.ones = sb("ones", [P, P])
        self.vecs = sb("vecs", [P, ROWS])
        self.bq_scaled = sb("bq_scaled", [P, KT])
        self.mod = sb("mod", [P, B, 4 * KT])
        self.gates = sb("gates", [P, B, 4, H])
        self.q_parts = nc.dram_tensor("q_parts", [B * G, P, 2, S], F32, kind="Internal").ap()
        self.k_parts = nc.dram_tensor("k_parts", [B * G, P, 2, S], F32, kind="Internal").ap()
        self.v_rows = nc.dram_tensor("v_rows", [B * S, H], F32, kind="Internal").ap()
        self.y_cols = nc.dram_tensor("y_cols", [B * G, P, S], F32, kind="Internal").ap()


def project(nc, sh, x, c, Wc, bc, Wq, bq, Wk, bk, Wv, bv, b1, bo, b2):
    with ExitStack() as ctx:
        def sb(name, shape, dt=F32):
            return ctx.enter_context(nc.sbuf_tensor(name, shape, dt))

        def pb(name, shape):
            return ctx.enter_context(nc.psum_tensor(name, shape, F32))

        def sem(name):
            return ctx.enter_context(nc.semaphore(name))

        rows = sb("rows", [ROWS, P])
        c_silu = sb("c_silu", [P, B * KT])
        c_wide = sb("c_wide", [P, B * KT, P])
        w_raw = sb("w_raw", [P, 2, KT, H])
        w_hi = sb("w_hi", [P, 3, KT, H], F32R)
        w_lo = sb("w_lo", [P, 3, KT, H], F32R)
        wc = sb("wc", [P, 4, KT, H])
        bc_wide = sb("bc_wide", [P, 4, H])
        xb = sb("xb", [P, 2, TT, H])
        stats = sb("stats", [P, TT, 6])
        mv = sb("mv", [P, TT, 2])
        var_eps = sb("var_eps", [P, TT])
        rstd = sb("rstd", [P, TT])
        neg_half = sb("neg_half", [P, TT])
        xm = sb("xm", [P, 2, TOK])
        xm_hi = sb("xm_hi", [P, 2, KT, TOK], F32R)
        xm_lo = sb("xm_lo", [P, 2, KT, TOK], F32R)
        qk = sb("qk", [P, 2, TOK])
        qk_out = sb("qk_out", [P, 4, 2, TOK], F32R)
        v_out = sb("v_out", [P, 2, H])

        mm_bank = [pb(f"mm_bank{n}", [P, TOK]) for n in range(4)]
        t_bank = [pb(f"t_bank{n}", [P, TOK]) for n in range(2)]
        c_bank = pb("c_bank", [P, H])
        g_bank = pb("g_bank", [P, H])

        rows_in, w_in, wide_in = sem("rows_in"), [sem(f"w_in{n}") for n in range(3)], sem("wide_in")
        wc_in = [sem(f"wc_in{n}") for n in range(6)]
        x_in = [sem(f"x_in{n}") for n in range(2)]
        const_ready, rows_t, vecs_ready = sem("const_ready"), sem("rows_t"), sem("vecs_ready")
        silu_ready, wide_ready = sem("silu_ready"), sem("wide_ready")
        c_done, c_taken, g_done, g_taken = sem("c_done"), sem("c_taken"), sem("g_done"), sem("g_taken")
        w_split = sem("w_split")
        stats_ready, rstd_ready, xn_ready = sem("stats_ready"), sem("rstd_ready"), sem("xn_ready")
        t_done, t_taken, xm_split = sem("t_done"), sem("t_taken"), sem("xm_split")
        mm_done, mm_taken, qk_split = sem("mm_done"), sem("mm_taken"), sem("qk_split")
        qk_stored = [sem(f"qk_stored{n}") for n in range(4)]
        v_stored = [sem(f"v_stored{n}") for n in range(2)]
        dve = sem("dve")
        norm_step, stats_seen, hi_step, qk_hi_step = sem("norm_step"), sem("stats_seen"), sem("hi_step"), sem("qk_hi_step")

        x_blocks = x.rearrange("b (n t p) d -> (b n) p t d", t=TT, p=P)
        v_blocks = sh.v_rows.rearrange("(n t p) d -> n t p d", t=TT, p=P)
        wc_parts = Wc.rearrange("(t p) (c n) -> c p t n", p=P, n=H)
        PER_BLOCK = 2 * G + TT
        N_QK = 2 * G
        block = ctx.enter_context(nc.Block())

        @block.sync
        def _(sp):
            for r, v, n in ((ROW_BC, bc, 6 * KT), (ROW_BQ, bq, KT), (ROW_BK, bk, KT), (ROW_BV, bv, KT), (ROW_B1, b1, MT)):
                sp.dma_start(rows[r:r + n, :], v.rearrange("(r p) -> r p", p=P)).then_inc(rows_in, 16)
            sp.dma_start(rows[ROW_C:ROWS, :], c.rearrange("b (t p) -> (b t) p", p=P)).then_inc(rows_in, 16)
            sp.dma_start(xb[:, 0, :, :], x_blocks[0]).then_inc(x_in[0], 16)
            for part in range(2):
                sp.dma_start(wc[:, part, :, :], wc_parts[part]).then_inc(wc_in[part], 16)
            for n, w in enumerate((Wq, Wk)):
                sp.dma_start(w_raw[:, n, :, :], w.rearrange("(t p) n -> p t n", p=P)).then_inc(w_in[n], 16)
            sp.dma_start(xb[:, 1, :, :], x_blocks[1]).then_inc(x_in[1], 16)
            for part in (2, 3):
                sp.dma_start(wc[:, part, :, :], wc_parts[part]).then_inc(wc_in[part], 16)
            for n, v in enumerate((bc[2 * H:3 * H], bc[5 * H:6 * H], bo, b2)):
                sp.dma_start(bc_wide[:, n, :], v.rearrange("(a n) -> a n", a=1).broadcast_to([P, H])).then_inc(wide_in, 16)
            sp.wait_ge(c_done, 2)
            for part in (4, 5):
                sp.dma_start(wc[:, part - 4, :, :], wc_parts[part]).then_inc(wc_in[part], 16)
            sp.wait_ge(w_split, 1)
            sp.dma_start(w_raw[:, 0, :, :], Wv.rearrange("(t p) n -> p t n", p=P)).then_inc(w_in[2], 16)

            def store(k, i, q, load_next):
                for m in range(N_QK):
                    dst = (sh.q_parts, sh.k_parts)[m % 2]
                    group, tok = sp.snap(k // BPB * G + m // 2), sp.snap(k % BPB * TOK)
                    sp.wait_ge(qk_split, 2 + N_QK * k + m + 1)
                    sp.dma_start(dst[bass.ds(group, 1), :, :, bass.ds(tok, TOK)].rearrange("a p s n -> p (a s) n"),
                                 qk_out[:, m % 4, :, :].bitcast(F32)).then_inc(qk_stored[m % 4], 16)
                    if m == N_QK // 2 and load_next:
                        sp.wait_ge(t_done, KT * (k + 1) + 1)
                        sp.dma_start(xb[:, q, :, :], x_blocks[k + 2]).then_inc(x_in[q], 16)
                for t in range(TT):
                    sp.wait_ge(mm_taken, 4 + PER_BLOCK * k + N_QK + t + 1)
                    sp.dma_start(v_blocks[k, t], v_out[:, t % 2, :]).then_inc(v_stored[t % 2], 16)

            with sp.Fori(0, NBLK // 2 - 1) as i:
                for q in range(2):
                    store(2 * i + q, i, q, True)
            for q in range(2):
                store(NBLK - 2 + q, NBLK // 2 - 1, q, False)
            for s in qk_stored:
                sp.wait_ge(s, 1 + 16 * NBLK * N_QK // 4)
            for s in v_stored:
                sp.wait_ge(s, 1 + 16 * NBLK * TT // 2)

        @block.gpsimd
        def _(pool):
            for s, n in ((t_taken, 2), (xm_split, 2), (mm_taken, 4), (qk_split, 2), (mm_done, 1)):
                pool.sem_inc(s, n)
            for s in qk_stored + v_stored:
                pool.sem_inc(s, 1)
            pool.memset(sh.ones[:, :], 1.0).then_inc(const_ready, 1)
            pool.memset(neg_half[:, :], -0.5).then_inc(const_ready, 1)
            pool.memset(sh.ident[:, :], 0.0).then_inc(const_ready, 1)
            pool.wait_ge(const_ready, 3)
            pool.affine_select(out=sh.ident[:, :], in_=sh.ident[:, :], compare_op=ALU.not_equal, fill=1.0,
                               base=0, pattern=[[-1, P]], channel_multiplier=1).then_inc(const_ready, 1)

            def root(k):
                pool.wait_ge(stats_ready, k + 1)
                pool.tensor_tensor(rstd[:, :], var_eps[:, :], neg_half[:, :], ALU.pow).then_inc(rstd_ready, 1)

            root(0)
            with pool.Fori(1, NBLK) as k:
                root(k)

        @block.vector
        def _(v):
            steps = [0]

            def after(ins):
                steps[0] += 1
                ins.then_inc(dve, 1)
                v.wait_ge(dve, steps[0])

            def norm(k, i, q):
                v.wait_ge(x_in[q], 16 * i + 16)
                for t in range(TT):
                    last = v.bn_stats(stats[:, t, :], xb[:, q, t, :])
                last.then_inc(norm_step, 1)
                v.wait_ge(norm_step, 2 * k + 1)
                v.sem_inc(stats_seen, 1)
                for t in range(TT):
                    last = v.bn_aggr(mv[:, t, :], stats[:, t, :])
                last.then_inc(norm_step, 1)
                v.wait_ge(norm_step, 2 * k + 2)
                v.tensor_scalar(var_eps[:, :], mv[:, :, 1], EPS, None, ALU.add).then_inc(stats_ready, 1)
                v.wait_ge(rstd_ready, k + 1)
                for t in range(TT):
                    last = v.tensor_scalar(xb[:, q, t, :], xb[:, q, t, :], mv[:, t, 0:1], rstd[:, t:t + 1],
                                           ALU.subtract, ALU.mult)
                last.then_inc(xn_ready, 1)

            def split_xm(k, q):
                v.wait_ge(mm_done, PER_BLOCK * (k - 1) + 1) if not isinstance(k, int) or k > 1 else None
                for t in range(KT):
                    v.wait_ge(t_taken, 2 + KT * k + t + 1)
                    v.tensor_copy(xm_hi[:, q, t, :], xm[:, t % 2, :]).then_inc(hi_step, 1)
                    v.wait_ge(hi_step, KT * k + t + 1)
                    v.tensor_tensor(xm_lo[:, q, t, :], xm[:, t % 2, :], xm_hi[:, q, t, :].bitcast(F32),
                                    ALU.subtract).then_inc(xm_split, 1)

            def split_qk(k, ms):
                for m in ms:
                    v.wait_ge(mm_taken, 4 + PER_BLOCK * k + m + 1)
                    v.wait_ge(qk_stored[m % 4], 16 * (k * N_QK // 4 + m // 4) + 1)
                    v.tensor_copy(qk_out[:, m % 4, 0, :], qk[:, m % 2, :]).then_inc(qk_hi_step, 1)
                    v.wait_ge(qk_hi_step, N_QK * k + m + 1)
                    v.tensor_tensor(qk_out[:, m % 4, 1, :], qk[:, m % 2, :], qk_out[:, m % 4, 0, :].bitcast(F32),
                                    ALU.subtract).then_inc(qk_split, 1)

            v.wait_ge(rows_t, 1)
            after(v.tensor_copy(sh.vecs[:, :], c_bank[:, 0:ROWS]))
            v.tensor_scalar(sh.bq_scaled[:, :], sh.vecs[:, ROW_BQ:ROW_BQ + KT], 1.0 / DH, None, ALU.mult).then_inc(vecs_ready, 1)
            norm(0, 0, 0)

            def mod_columns(part, column, one):
                v.wait_ge(c_done, {0: 1, 1: 2, 3: 3, 4: 4}[part])
                for b in range(B):
                    last = v.tensor_tensor(sh.mod[:, b, column:column + KT], c_bank[:, :].rearrange("p (t b) -> p b t", t=H // 2)[:, b, 0:KT],
                                           sh.vecs[:, ROW_BC + part * KT:ROW_BC + (part + 1) * KT], ALU.add)
                if one:
                    after(last)
                    last = v.tensor_scalar(sh.mod[:, :, column:column + KT], sh.mod[:, :, column:column + KT], 1.0, None, ALU.add)
                last.then_inc(c_taken, 1)

            mod_columns(0, SHIFT_MSA, False)
            mod_columns(1, SCALE_MSA, True)
            split_xm(0, 0)
            for n in range(3):
                v.wait_ge(w_in[n], 16)
                after(v.tensor_copy(w_hi[:, n, :, :], w_raw[:, n % 2, :, :]))
                v.tensor_tensor(w_lo[:, n, :, :], w_raw[:, n % 2, :, :], w_hi[:, n, :, :].bitcast(F32), ALU.subtract).then_inc(w_split, 1)
            v.wait_ge(silu_ready, 1)
            for n in range(B * KT):
                last = v.tensor_scalar(c_wide[:, n, :], sh.ones[:, :], c_silu[:, n:n + 1], None, ALU.mult)
            last.then_inc(wide_ready, 1)

            def body(k, i, q, has_next):
                if has_next:
                    norm(k + 1, i + q, 1 - q)
                split_qk(k, range(N_QK // 2))
                if has_next:
                    split_xm(k + 1, 1 - q)
                split_qk(k, range(N_QK // 2, N_QK))

            with v.Fori(0, NBLK // 2 - 1) as i:
                for q in range(2):
                    body(2 * i + q, i, q, True)
            body(NBLK - 2, NBLK // 2 - 1, 0, True)
            body(NBLK - 1, NBLK // 2 - 1, 1, False)

            mod_columns(3, SHIFT_MLP, False)
            mod_columns(4, SCALE_MLP, True)
            v.wait_ge(wide_in, 16 * 4)
            n = 0
            for part, gate, bias, wide in ((2, G_MSA, GBO, 0), (5, G_MLP, GB2, 1)):
                for b in range(B):
                    n += 1
                    v.wait_ge(g_done, n)
                    after(v.tensor_tensor(sh.gates[:, b, gate, :], g_bank[:, :], bc_wide[:, wide, :], ALU.add))
                    v.tensor_tensor(sh.gates[:, b, bias, :], sh.gates[:, b, gate, :], bc_wide[:, 2 + wide, :], ALU.mult).then_inc(g_taken, 1)

        @block.scalar
        def _(act):
            act.wait_ge(vecs_ready, 1)
            act.activation(c_silu[:, :], sh.vecs[:, ROW_C:ROWS], ACT.Silu).then_inc(silu_ready, 1)

            def modulate(k, b, t0=0):
                for t in range(KT):
                    act.wait_ge(t_done, KT * k + t + 1)
                    act.wait_ge(xm_split, KT * k + t + 1)
                    act.activation(xm[:, t % 2, :], t_bank[t % 2][:, :], ACT.Identity,
                                   scale=sh.mod[:, bass.ds(b, 1), SCALE_MSA + t].rearrange("p a -> p (a)"),
                                   bias=sh.mod[:, bass.ds(b, 1), SHIFT_MSA + t].rearrange("p a -> p (a)")).then_inc(t_taken, 1)

            def take_qk(k, ms):
                for m in ms:
                    act.wait_ge(mm_done, 1 + PER_BLOCK * k + m + 1)
                    act.wait_ge(qk_split, N_QK * k + m + 1)
                    g = m // 2
                    if m % 2 == 0:
                        ins = act.activation(qk[:, 0, :], mm_bank[m % 4][:, :], ACT.Identity,
                                             scale=1.0 / DH, bias=sh.bq_scaled[:, g:g + 1])
                    else:
                        ins = act.activation(qk[:, 1, :], mm_bank[m % 4][:, :], ACT.Identity,
                                             bias=sh.vecs[:, ROW_BK + g:ROW_BK + g + 1])
                    ins.then_inc(mm_taken, 1)

            def body(k, next_b, has_next):
                take_qk(k, range(N_QK // 2))
                if has_next:
                    modulate(k + 1, next_b)
                take_qk(k, range(N_QK // 2, N_QK))
                for t in range(TT):
                    act.wait_ge(mm_done, 1 + PER_BLOCK * k + N_QK + t + 1)
                    act.wait_ge(v_stored[t % 2], 16 * (k * TT // 2 + t // 2) + 1)
                    act.activation(v_out[:, t % 2, :], mm_bank[(N_QK + t) % 4][:, :], ACT.Copy).then_inc(mm_taken, 1)

            act.wait_ge(c_taken, 2)
            modulate(0, 0)
            with act.Fori(0, NBLK // 2 - 1) as i:
                for q in range(2):
                    body(2 * i + q, (2 * i + q + 1) // BPB, True)
            body(NBLK - 2, B - 1, True)
            body(NBLK - 1, 0, False)

        @block.tensor
        def _(pe):
            pe.wait_ge(rows_in, 16 * 6)
            pe.wait_ge(const_ready, 4)
            pe.transpose(c_bank[:, 0:ROWS], rows[:, :], sh.ident[0:ROWS, 0:ROWS]).then_inc(rows_t, 1)

            def columns(part):
                pe.wait_ge(wc_in[part], 16)
                for t in range(KT):
                    for s in range(KT):
                        last = pe.matmul(c_bank[:, t * B:(t + 1) * B], wc[:, part % 4, s, t * P:(t + 1) * P],
                                         c_silu[:, :].rearrange("p (b s) -> p s b", s=KT)[:, s, :],
                                         start=(s == 0), stop=(s == KT - 1))
                last.then_inc(c_done, 1)

            def transposes(k, q):
                pe.wait_ge(xn_ready, k + 1)
                for t in range(KT):
                    pe.wait_ge(t_taken, KT * k + t + 1)
                    for s in range(TT):
                        last = pe.transpose(t_bank[t % 2][:, s * P:(s + 1) * P], xb[:, q, s, t * P:(t + 1) * P], sh.ident[:, :])
                    last.then_inc(t_done, 1)

            def three(bank, hi_l, lo_l, hi_r, lo_r):
                for t in range(KT):
                    pe.matmul(bank, hi_l(t), hi_r(t), start=(t == 0), stop=False)
                    pe.matmul(bank, hi_l(t), lo_r(t), start=False, stop=False)
                    last = pe.matmul(bank, lo_l(t), hi_r(t), start=False, stop=(t == KT - 1))
                last.then_inc(mm_done, 1)

            def products(k, q, ms):
                for m in ms:
                    pe.wait_ge(mm_taken, PER_BLOCK * k + m + 1)
                    bank = mm_bank[m % 4][:, :]
                    if m < N_QK:
                        n, g = m % 2, m // 2
                        three(bank, lambda t: w_hi[:, n, t, g * P:(g + 1) * P], lambda t: w_lo[:, n, t, g * P:(g + 1) * P],
                              lambda t: xm_hi[:, q, t, :], lambda t: xm_lo[:, q, t, :])
                    else:
                        s = m - N_QK
                        three(bank, lambda t: xm_hi[:, q, t, s * P:(s + 1) * P], lambda t: xm_lo[:, q, t, s * P:(s + 1) * P],
                              lambda t: w_hi[:, 2, t, :], lambda t: w_lo[:, 2, t, :])

            def body(k, q, has_next):
                pe.wait_ge(xm_split, 2 + KT * (k + 1))
                products(k, q, range(N_QK // 2))
                if has_next:
                    transposes(k + 1, 1 - q)
                products(k, q, range(N_QK // 2, PER_BLOCK))

            pe.wait_ge(silu_ready, 1)
            columns(0)
            pe.wait_ge(c_taken, 1)
            columns(1)
            transposes(0, 0)
            pe.wait_ge(w_split, 3)
            with pe.Fori(0, NBLK // 2 - 1) as i:
                for q in range(2):
                    body(2 * i + q, q, True)
            body(NBLK - 2, 0, True)
            body(NBLK - 1, 1, False)

            pe.wait_ge(c_taken, 2)
            columns(3)
            pe.wait_ge(c_taken, 3)
            columns(4)
            pe.wait_ge(wide_ready, 1)
            n = 0
            for part in (2, 5):
                pe.wait_ge(wc_in[part], 16)
                for b in range(B):
                    if n:
                        pe.wait_ge(g_taken, n)
                    n += 1
                    for s in range(KT):
                        last = pe.matmul(g_bank[:, :], c_wide[:, b * KT + s, :], wc[:, part % 4, s, :],
                                         start=(s == 0), stop=(s == KT - 1))
                    last.then_inc(g_done, 1)


STACK = 3 * DH
Q_PARTS, K_PARTS = (0, 0, 1), (0, 1, 0)
N_IT = B * G * BPB
N_MAX = BPB * HPG * TT
CHUNK = TOK // P
N_PAIR = NKT // 2


def attend(nc, sh):
    with ExitStack() as ctx:
        def sb(name, shape, dt=F32):
            return ctx.enter_context(nc.sbuf_tensor(name, shape, dt))

        def pb(name, shape):
            return ctx.enter_context(nc.psum_tensor(name, shape, F32))

        def sem(name):
            return ctx.enter_context(nc.semaphore(name))

        km = sb("km", [STACK, HPG, S], F32R)
        ks = sb("ks", [STACK + 1, HPG, S], F32R)
        qm = sb("qm", [STACK, HPG, TOK], F32R)
        qs = [sb(f"qs{u}", [STACK + 1, HPG, TOK], F32R) for u in range(2)]
        vs = sb("vs", [P, NKT, P])
        probs = sb("probs", [P, 4, HPG, TOK])
        pair_sum = sb("pair_sum", [P, 2, HPG, TOK])
        part_max = sb("part_max", [P, HPG * TT, BPB])
        neg_max = sb("neg_max", [P, HPG * TT])
        neg_max_row = sb("neg_max_row", [HPG * TT, P], F32R)
        y_raw = sb("y_raw", [P, 2, TOK])
        inv = sb("inv", [P, TOK])
        y_out = sb("y_out", [P, 2, TOK])

        s_pair = [pb(f"s_pair{n}", [P, 2, TOK]) for n in range(2)]
        y_bank = pb("y_bank", [P, TOK])
        d_bank = pb("d_bank", [P, TOK])
        m_bank = [pb(f"m_bank{n}", [P, TOK]) for n in range(2)]

        km_in = [sem(f"km_in{c}") for c in range(BPB)]
        ks_in = [sem(f"ks_in{c}") for c in range(BPB)]
        v_in = [sem(f"v_in{c}") for c in range(BPB)]
        qm_in = sem("qm_in")
        qs_in = [sem(f"qs_in{u}") for u in range(2)]
        row_in = [sem(f"row_in{u}") for u in range(2)]
        ones_row = sem("ones_row")
        s_done, p_done, av_done, pair_ready, d_done = sem("s_done"), sem("p_done"), sem("av_done"), sem("pair_ready"), sem("d_done")
        y_taken, d_taken, y_normed, inv_ready = sem("y_taken"), sem("d_taken"), sem("y_normed"), sem("inv_ready")
        y_stored = [sem(f"y_stored{u}") for u in range(2)]
        m_done, m_taken, neg_ready = sem("m_done"), sem("m_taken"), sem("neg_ready")
        M_USES = N_MAX + 1

        by_head = "a (h c) n -> c (a h) n"
        block = ctx.enter_context(nc.Block())

        @block.sync
        def _(sp):
            def load_rows(dst, src, parts, group, part_tok, n, done):
                for r, part in enumerate(parts):
                    sp.dma_start(dst(r), src[bass.ds(group, 1), :, part, part_tok:part_tok + n].rearrange(by_head, c=DH)).then_inc(done, 16)

            def load_km(group, c):
                load_rows(lambda r: km[r * DH:(r + 1) * DH, :, c * TOK:(c + 1) * TOK].bitcast(F32), sh.k_parts, K_PARTS, group, c * TOK, TOK, km_in[c])

            def load_ks(group, c):
                load_rows(lambda r: ks[r * DH:(r + 1) * DH, :, c * TOK:(c + 1) * TOK].bitcast(F32), sh.k_parts, K_PARTS, group, c * TOK, TOK, ks_in[c])

            def load_v(group, c):
                row, col = sp.snap(group // G * S + c * TOK), sp.snap(group % G * P)
                sp.dma_start(vs[:, c * CHUNK:(c + 1) * CHUNK, :],
                             sh.v_rows[bass.ds(row, TOK), bass.ds(col, P)].rearrange("(t p) n -> p t n", p=P)).then_inc(v_in[c], 16)

            def load_qm(group, qt):
                load_rows(lambda r: qm[r * DH:(r + 1) * DH, :, :].bitcast(F32), sh.q_parts, Q_PARTS, group, qt * TOK, TOK, qm_in)

            def load_qs(group, qt):
                u = qt % 2
                load_rows(lambda r: qs[u][r * DH:(r + 1) * DH, :, :].bitcast(F32), sh.q_parts, Q_PARTS, group, qt * TOK, TOK, qs_in[u])

            def load_row(u):
                sp.dma_start(qs[u][STACK:STACK + 1, :, :].rearrange("a h n -> a (h n)").bitcast(F32),
                             neg_max_row[:, :].bitcast(F32)).then_inc(row_in[u], 16)

            def iteration(group, qt, last_group):
                i = BPB * group + qt
                following = [(group + (qt + d) // BPB, (qt + d) % BPB) for d in (1, 2)]
                there = [not (last_group and qt + d >= BPB) for d in (1, 2)]
                if there[0]:
                    sp.wait_ge(s_done, 1 + 2 * NKT * i)
                    load_qs(*following[0])
                for c in range(BPB - 1 if qt == BPB - 1 else BPB):
                    if qt == BPB - 2 and not last_group:
                        sp.wait_ge(m_done, M_USES * (i + 1) + HPG * TT * (c + 1))
                        load_km(group + 1, c)
                    if qt == BPB - 1 and not last_group:
                        sp.wait_ge(s_done, 1 + 2 * NKT * i + 2 * CHUNK * (c + 1))
                        load_ks(group + 1, c)
                        sp.wait_ge(av_done, 4 + NKT * i + CHUNK * (c + 1))
                        load_v(group + 1, c)
                if there[1]:
                    sp.wait_ge(m_done, M_USES * (i + 1) + N_MAX)
                    load_qm(*following[1])
                if there[0]:
                    sp.wait_ge(m_taken, 2 + M_USES * (i + 2))
                    load_row((qt + 1) % 2)
                if qt == BPB - 1 and not last_group:
                    c = BPB - 1
                    sp.wait_ge(s_done, 1 + 2 * NKT * (i + 1))
                    load_ks(group + 1, c)
                    sp.wait_ge(av_done, 4 + NKT * (i + 1))
                    load_v(group + 1, c)

            load_qm(0, 0)
            for c in range(BPB):
                load_km(0, c)
            load_qs(0, 0)
            for c in range(BPB):
                load_ks(0, c)
                load_v(0, c)
            sp.wait_ge(m_done, N_MAX)
            load_qm(0, 1)
            sp.wait_ge(m_taken, 2 + M_USES)
            load_row(0)
            with sp.Fori(0, B * G - 1) as group:
                for qt in range(BPB):
                    iteration(group, qt, False)
            for qt in range(BPB):
                iteration(B * G - 1, qt, True)
            for u in range(2):
                sp.wait_ge(y_stored[u], 1 + 16 * N_IT // 2)

        @block.gpsimd
        def _(pool):
            for s, n in ((s_done, 1), (p_done, 2), (av_done, 4), (pair_ready, 2), (d_done, 2), (y_taken, 1),
                         (d_taken, 1), (y_normed, 2), (m_taken, 2), (y_stored[0], 1), (y_stored[1], 1)):
                pool.sem_inc(s, n)
            pool.memset(ks[STACK:STACK + 1, :, :].bitcast(F32), 1.0).then_inc(ones_row, 1)
            with pool.Fori(0, N_IT) as i:
                for j in range(N_PAIR):
                    pool.wait_ge(d_done, N_PAIR * i + j + 1)
                    for r in range(2):
                        pool.wait_ge(p_done, 2 + 2 * NKT * i + 4 * j + 3 + r)
                        ins = pool.tensor_tensor(pair_sum[:, j % 2, 2 * r:2 * r + 2, :], probs[:, 2 * j % 4, 2 * r:2 * r + 2, :],
                                                 probs[:, (2 * j + 1) % 4, 2 * r:2 * r + 2, :], ALU.add)
                    ins.then_inc(pair_ready, 1)

        @block.scalar
        def _(act):
            def take_y(i, u):
                act.wait_ge(av_done, 4 + NKT * (i + 1))
                act.wait_ge(y_normed, i + 1)
                act.activation(y_raw[:, u, :], y_bank[:, :], ACT.Copy).then_inc(y_taken, 1)

            def store_y(i, u):
                group, tok = act.snap(i // BPB), act.snap(i % BPB * TOK)
                act.wait_ge(y_normed, 2 + i + 1)
                act.dma_start(sh.y_cols[bass.ds(group, 1), :, bass.ds(tok, TOK)].rearrange("a p n -> p (a n)"),
                              y_out[:, u, :]).then_inc(y_stored[u], 16)

            def body(i, u, has_prev):
                for t in range(NKT):
                    for r in range(2):
                        act.wait_ge(s_done, 1 + 2 * NKT * i + 2 * t + r + 1)
                        if r == 0:
                            act.wait_ge(av_done, NKT * i + t + 1)
                            act.wait_ge(pair_ready, N_PAIR * i + t // 2 + 1)
                        act.activation(probs[:, t % 4, 2 * r:2 * r + 2, :], s_pair[r][:, :, :], ACT.Exp).then_inc(p_done, 1)
                    if t == 0 and has_prev:
                        take_y(i - 1, 1 - u)
                    if t == 8 and has_prev:
                        store_y(i - 1, 1 - u)

            body(0, 0, False)
            with act.Fori(0, N_IT // 2 - 1) as j:
                body(2 * j + 1, 1, True)
                body(2 * j + 2, 0, True)
            body(N_IT - 1, 1, True)
            take_y(N_IT - 1, 1)
            store_y(N_IT - 1, 1)

        @block.vector
        def _(v):
            def maxima(i, row_before=None, middle=None):
                for n in range(N_MAX):
                    c, hs = n // (HPG * TT), n % (HPG * TT)
                    v.wait_ge(m_done, M_USES * i + n + 1)
                    v.tensor_reduce(part_max[:, hs, c:c + 1], m_bank[n % 2][:, :], AX.X, ALU.max).then_inc(m_taken, 1)
                    if n == 22 and middle is not None:
                        middle()
                v.wait_ge(m_taken, 2 + M_USES * i + N_MAX)
                v.tensor_reduce(neg_max[:, :], part_max[:, :, :], AX.X, ALU.max, negate=True).then_inc(neg_ready, 1)
                v.wait_ge(m_done, M_USES * (i + 1))
                if row_before is not None:
                    v.wait_ge(*row_before)
                v.tensor_copy(neg_max_row[:, :], m_bank[0][0:HPG * TT, 0:P]).then_inc(m_taken, 1)

            def normalise(i, u):
                v.wait_ge(d_done, 2 + N_PAIR * (i + 1))
                v.reciprocal(inv[:, :], d_bank[:, :]).then_inc(d_taken, 1)
                v.wait_ge(y_taken, 1 + i + 1)
                v.wait_ge(y_stored[u], 16 * (i // 2) + 1)
                v.wait_ge(d_taken, 1 + i + 1)
                v.tensor_tensor(y_out[:, u, :], y_raw[:, u, :], inv[:, :], ALU.mult).then_inc(y_normed, 1)

            def body(i, u, has_prev):
                maxima(i + 1, (row_in[u], 16 * (i // 2 + 1)), (lambda: normalise(i - 1, 1 - u)) if has_prev else None)

            maxima(0)
            body(0, 0, False)
            with v.Fori(0, N_IT // 2 - 1) as j:
                body(2 * j + 1, 1, True)
                body(2 * j + 2, 0, True)
            normalise(N_IT - 2, 0)
            normalise(N_IT - 1, 1)

        @block.tensor
        def _(pe):
            def max_product(i, group, n):
                c, h, s = n // (HPG * TT), n // TT % HPG, n % TT
                if n == 0:
                    pe.wait_ge(qm_in, 16 * 3 * (i + 1))
                if n % (HPG * TT) == 0:
                    pe.wait_ge(km_in[c], 16 * 3 * (group + 1))
                pe.wait_ge(m_taken, M_USES * i + n + (2 if n == 0 else 1))
                pe.matmul(m_bank[n % 2][:, :], qm[:, h, s * P:(s + 1) * P], km[:, h, c * TOK:(c + 1) * TOK],
                          start=True, stop=True).then_inc(m_done, 1)

            def max_transpose(i):
                pe.wait_ge(neg_ready, i + 1)
                pe.wait_ge(m_taken, M_USES * i + N_MAX + 1)
                pe.transpose(m_bank[0][0:HPG * TT, 0:P], neg_max[:, :], sh.ident[:, :]).then_inc(m_done, 1)

            def scores(i, group, t):
                if t % CHUNK == 0:
                    pe.wait_ge(ks_in[t // CHUNK], 16 * 3 * (group + 1))
                for r in range(2):
                    pe.wait_ge(p_done, 2 * NKT * i + 2 * t + r + 1)
                    for h in (2 * r, 2 * r + 1):
                        last = pe.matmul(s_pair[r][:, h % 2, :], ks[:, h, t * P:(t + 1) * P], q_now(h), start=True, stop=True)
                    last.then_inc(s_done, 1)

            def times_v(i, group, t):
                if t % CHUNK == 0:
                    pe.wait_ge(v_in[t // CHUNK], 16 * (group + 1))
                if t == 0:
                    pe.wait_ge(y_taken, i + 1)
                pe.wait_ge(p_done, 2 + 2 * NKT * i + 2 * t + 2)
                for h in range(HPG):
                    last = pe.matmul(y_bank[h * DH:(h + 1) * DH, :], vs[:, t, h * DH:(h + 1) * DH], probs[:, t % 4, h, :],
                                     start=(t == 0), stop=(t == NKT - 1))
                last.then_inc(av_done, 1)

            def sums(i, j):
                if j == 0:
                    pe.wait_ge(d_taken, i + 1)
                pe.wait_ge(pair_ready, 2 + N_PAIR * i + j + 1)
                for h in range(HPG):
                    last = pe.matmul(d_bank[h * DH:(h + 1) * DH, :], sh.ones[:, 0:DH], pair_sum[:, j % 2, h, :],
                                     start=(j == 0), stop=(j == N_PAIR - 1))
                last.then_inc(d_done, 1)

            state = {}

            def q_now(h):
                return qs[state["u"]][:, h, :]

            def body(i, u, has_prev, has_next):
                state["u"] = u
                group = i // BPB
                pe.wait_ge(qs_in[u], 16 * 3 * (i // 2 + 1))
                pe.wait_ge(row_in[u], 16 * (i // 2 + 1))
                left = list(range(N_MAX)) if has_next else []
                for t in range(NKT):
                    scores(i, group, t)
                    for n in left[:5]:
                        max_product(i + 1, (i + 1) // BPB, n)
                    left = left[5:]
                    if t > 0:
                        times_v(i, group, t - 1)
                    elif has_prev:
                        times_v(i - 1, (i - 1) // BPB, NKT - 1)
                    if t % 2 == 0 and t >= 4:
                        sums(i, t // 2 - 2)
                    elif t in (0, 2) and has_prev:
                        sums(i - 1, N_PAIR - 2 + t // 2)
                    if t == 14 and has_next:
                        max_transpose(i + 1)

            for n in range(N_MAX):
                max_product(0, 0, n)
            max_transpose(0)
            pe.wait_ge(ones_row, 1)
            body(0, 0, False, True)
            with pe.Fori(0, N_IT // 2 - 1) as j:
                body(2 * j + 1, 1, True, True)
                body(2 * j + 2, 0, True, True)
            body(N_IT - 1, 1, True, False)
            times_v(N_IT - 1, B * G - 1, NKT - 1)
            sums(N_IT - 1, N_PAIR - 2)
            sums(N_IT - 1, N_PAIR - 1)


def feed_forward(nc, sh, x, Wo, W1, W2, out):
    with ExitStack() as ctx:
        def sb(name, shape, dt=F32):
            return ctx.enter_context(nc.sbuf_tensor(name, shape, dt))

        def pb(name, shape):
            return ctx.enter_context(nc.psum_tensor(name, shape, F32))

        def sem(name):
            return ctx.enter_context(nc.semaphore(name))

        w1_raw = sb("w1_raw", [P, KT, MLP])
        w2_raw = sb("w2_raw", [P, MT, H])
        w1_hi, w1_lo = sb("w1_hi", [P, 2, KT, P], F32R), sb("w1_lo", [P, 2, KT, P], F32R)
        w2_hi, w2_lo = sb("w2_hi", [P, 2, H], F32R), sb("w2_lo", [P, 2, H], F32R)
        wo_hi, wo_lo = sb("wo_hi", [P, KT, H], F32R), sb("wo_lo", [P, KT, H], F32R)
        yb = sb("yb", [P, KT, TOK])
        y_hi, y_lo = sb("y_hi", [P, KT, TOK], F32R), sb("y_lo", [P, KT, TOK], F32R)
        xb = sb("xb2", [P, 2, TT, H])
        stats, mv = sb("stats2", [P, TT, 6]), sb("mv2", [P, TT, 2])
        var_eps, rstd, neg_half = sb("var_eps2", [P, TT]), sb("rstd2", [P, TT]), sb("neg_half2", [P, TT])
        xn = sb("xn", [P, TT, H])
        xm = sb("xm2", [P, KT, TOK])
        xm_hi, xm_lo = sb("xm2_hi", [P, KT, TOK], F32R), sb("xm2_lo", [P, KT, TOK], F32R)
        h = sb("h", [P, 2, TOK])
        h_hi, h_lo = sb("h_hi", [P, 2, TOK], F32R), sb("h_lo", [P, 2, TOK], F32R)
        gated = sb("gated", [P, 2, H])

        acc_bank = [pb(f"acc_bank{t}", [P, H]) for t in range(TT)]
        up_bank = [pb(f"up_bank{n}", [P, TOK]) for n in range(2)]
        o_bank = pb("o_bank", [P, H])
        t_bank = pb("t_bank", [P, TOK])

        wo_in, w1_in, w2_in, y_in = sem("wo_in"), sem("w1_in"), sem("w2_in"), sem("y_in")
        x_in = [sem(f"x2_in{q}") for q in range(2)]
        stored = [sem(f"stored{q}") for q in range(2)]
        wo_hi_ready, wo_split, half_ready = sem("wo_hi_ready"), sem("wo_split"), sem("half_ready")
        y_biased, y_split, y_hi_step = sem("y_biased"), sem("y_split"), sem("y_hi_step")
        x_biased, wo_done, wo_taken, gated_step, x1_step = sem("x_biased"), sem("wo_done"), sem("wo_taken"), sem("gated_step"), sem("x1_step")
        norm_step, stats_seen, stats_ready, rstd_ready, xn_ready, x1_biased = (
            sem("norm_step2"), sem("stats_seen2"), sem("stats_ready2"), sem("rstd_ready2"), sem("xn_ready2"), sem("x1_biased"))
        t_done, t_taken, xm_hi_step, xm_split = sem("t_done2"), sem("t_taken2"), sem("xm_hi_step"), sem("xm_split2")
        up_done, up_taken, h_hi_step, h_split, down_done = sem("up_done"), sem("up_taken"), sem("h_hi_step"), sem("h_split"), sem("down_done")
        w1_hi_ready, w1_split, w2_hi_ready, w2_split = sem("w1_hi_ready"), sem("w1_split"), sem("w2_hi_ready"), sem("w2_split")
        acc_taken, acc_step, out_ready = sem("acc_taken"), sem("acc_step"), sem("out_ready")

        x_blocks = x.rearrange("b (n t p) d -> (b n) p t d", t=TT, p=P)
        out_blocks = out.rearrange("b (n t p) d -> (b n) t p d", t=TT, p=P)
        block = ctx.enter_context(nc.Block())

        def gate(b, which):
            return sh.gates[:, bass.ds(b, 1), which, :].rearrange("p a n -> p (a n)")

        @block.sync
        def _(sp):
            def load_y(k):
                group, tok = sp.snap(k // BPB * G), sp.snap(k % BPB * TOK)
                sp.dma_start(yb[:, :, :], sh.y_cols[bass.ds(group, G), :, bass.ds(tok, TOK)].rearrange("g p n -> p g n")).then_inc(y_in, 16)

            sp.dma_start(xn[:, :, :], Wo.rearrange("(t p) n -> p t n", p=P)).then_inc(wo_in, 16)
            sp.dma_start(yb[:, :, :], sh.y_cols[0:G, :, 0:TOK].rearrange("g p n -> p g n")).then_inc(y_in, 16)
            sp.dma_start(xb[:, 0, :, :], x_blocks[0]).then_inc(x_in[0], 16)
            for t in range(KT):
                sp.dma_start(w1_raw[:, t, :], W1[t * P:(t + 1) * P, :]).then_inc(w1_in, 16)
            sp.dma_start(xb[:, 1, :, :], x_blocks[1]).then_inc(x_in[1], 16)
            for n in range(4):
                sp.dma_start(w2_raw[:, n * MT // 4:(n + 1) * MT // 4, :],
                             W2[n * MLP // 4:(n + 1) * MLP // 4, :].rearrange("(j p) n -> p j n", p=P)).then_inc(w2_in, 16)
            sp.wait_ge(y_split, KT)
            load_y(1)

            def body(k, i, q, load_next):
                if load_next:
                    sp.wait_ge(y_split, KT * (k + 2))
                    load_y(k + 2)
                for t in range(TT):
                    sp.wait_ge(out_ready, TT * k + t + 1)
                    sp.dma_start(out_blocks[k, t], xb[:, q, t, :]).then_inc(stored[q], 16)
                if load_next:
                    sp.wait_ge(stored[q], 16 * TT * (i + 1))
                    sp.dma_start(xb[:, q, :, :], x_blocks[k + 2]).then_inc(x_in[q], 16)

            with sp.Fori(0, NBLK // 2 - 1) as i:
                for q in range(2):
                    body(2 * i + q, i, q, True)
            for q in range(2):
                body(NBLK - 2 + q, NBLK // 2 - 1, q, False)
            for q in range(2):
                sp.wait_ge(stored[q], 16 * TT * NBLK // 2)

        @block.gpsimd
        def _(pool):
            for s, n in ((wo_done, 1), (wo_taken, 1), (t_taken, 1), (xm_split, 4), (up_done, 2), (up_taken, 2),
                         (h_split, 2), (down_done, 2), (acc_taken, 4)):
                pool.sem_inc(s, n)
            pool.memset(neg_half[:, :], -0.5).then_inc(half_ready, 1)
            pool.wait_ge(half_ready, 1)

            def bias_x(k, i, q, b):
                pool.wait_ge(x_in[q], 16 * (i + 1))
                for t in range(TT):
                    pool.tensor_tensor(xb[:, q, t, :], xb[:, q, t, :], gate(b, GBO), ALU.add).then_inc(x_biased, 1)

            def root(k):
                pool.wait_ge(stats_ready, k + 1)
                pool.tensor_tensor(rstd[:, :], var_eps[:, :], neg_half[:, :], ALU.pow).then_inc(rstd_ready, 1)

            def bias_x1(k, q, b):
                pool.wait_ge(xn_ready, k + 1)
                for t in range(TT):
                    ins = pool.tensor_tensor(xb[:, q, t, :], xb[:, q, t, :], gate(b, GB2), ALU.add)
                ins.then_inc(x1_biased, 1)

            def split_w1(n, j):
                pool.wait_ge(w1_hi_ready, n + 1)
                pool.tensor_tensor(w1_lo[:, j % 2, :, :], w1_raw[:, :, j * P:(j + 1) * P], w1_hi[:, j % 2, :, :].bitcast(F32),
                                   ALU.subtract).then_inc(w1_split, 1)

            def split_w2(n, j):
                pool.wait_ge(w2_hi_ready, n + 1)
                pool.tensor_tensor(w2_lo[:, j % 2, :], w2_raw[:, j, :], w2_hi[:, j % 2, :].bitcast(F32), ALU.subtract).then_inc(w2_split, 1)

            def body(k, i, q, b, has_next):
                for j in range(MT):
                    n = MT * k + j
                    if has_next or j < MT - 2:
                        split_w1(n + 2, (j + 2) % MT)
                    if has_next or j < MT - 1:
                        split_w2(n + 1, (j + 1) % MT)
                    if has_next:
                        if j == 0:
                            bias_x(k + 1, i, 1 - q, b)
                        if j == 8:
                            root(k + 1)
                        if j == 9:
                            bias_x1(k + 1, 1 - q, b)

            bias_x(0, 0, 0, 0)
            root(0)
            bias_x1(0, 0, 0)
            split_w1(0, 0)
            split_w1(1, 1)
            split_w2(0, 0)
            with pool.Fori(0, NBLK // 2 - 1) as i:
                for q in range(2):
                    body(2 * i + q, i + q, q, (2 * i + q + 1) // BPB, True)
            body(NBLK - 2, NBLK // 2 - 1, 0, B - 1, True)
            body(NBLK - 1, 0, 1, B - 1, False)

        @block.vector
        def _(v):
            def split_y(k):
                v.wait_ge(wo_done, TT * k + 1)
                for g in range(G):
                    v.wait_ge(y_biased, G * k + g + 1)
                    v.tensor_copy(y_hi[:, g, :], yb[:, g, :]).then_inc(y_hi_step, 1)
                    v.wait_ge(y_hi_step, G * k + g + 1)
                    v.tensor_tensor(y_lo[:, g, :], yb[:, g, :], y_hi[:, g, :].bitcast(F32), ALU.subtract).then_inc(y_split, 1)

            def residual(k, q, b, t):
                n = TT * k + t
                v.wait_ge(wo_done, 1 + n + 1)
                v.tensor_tensor(gated[:, t % 2, :], o_bank[:, :], gate(b, G_MSA), ALU.mult).then_inc(wo_taken, 1)
                v.wait_ge(wo_taken, 1 + n + 1)
                v.wait_ge(x_biased, n + 1)
                v.tensor_tensor(xb[:, q, t, :], xb[:, q, t, :], gated[:, t % 2, :], ALU.add).then_inc(x1_step, 1)
                v.wait_ge(x1_step, n + 1)
                v.bn_stats(stats[:, t, :], xb[:, q, t, :]).then_inc(norm_step, 1)

            def variance(k):
                v.wait_ge(norm_step, (TT + 1) * k + TT)
                v.sem_inc(stats_seen, 1)
                for t in range(TT):
                    last = v.bn_aggr(mv[:, t, :], stats[:, t, :])
                last.then_inc(norm_step, 1)
                v.wait_ge(norm_step, (TT + 1) * (k + 1))
                v.tensor_scalar(var_eps[:, :], mv[:, :, 1], EPS, None, ALU.add).then_inc(stats_ready, 1)

            def normalise(k, q):
                v.wait_ge(rstd_ready, k + 1)
                for t in range(TT):
                    last = v.tensor_scalar(xn[:, t, :], xb[:, q, t, :], mv[:, t, 0:1], rstd[:, t:t + 1], ALU.subtract, ALU.mult)
                last.then_inc(xn_ready, 1)

            def split_xm(k):
                v.wait_ge(up_done, MT * k + 2)
                for t in range(KT):
                    v.wait_ge(t_taken, 1 + KT * k + t + 1)
                    v.tensor_copy(xm_hi[:, t, :], xm[:, t, :]).then_inc(xm_hi_step, 1)
                    v.wait_ge(xm_hi_step, KT * k + t + 1)
                    v.tensor_tensor(xm_lo[:, t, :], xm[:, t, :], xm_hi[:, t, :].bitcast(F32), ALU.subtract).then_inc(xm_split, 1)

            def high_w1(n, j):
                v.wait_ge(up_done, n + 1)
                v.tensor_copy(w1_hi[:, j % 2, :, :], w1_raw[:, :, j * P:(j + 1) * P]).then_inc(w1_hi_ready, 1)

            def high_w2(n, j):
                v.wait_ge(down_done, n + 1)
                v.tensor_copy(w2_hi[:, j % 2, :], w2_raw[:, j, :]).then_inc(w2_hi_ready, 1)

            def split_h(n, j):
                v.wait_ge(up_taken, 2 + n + 1)
                v.wait_ge(down_done, n + 1)
                v.tensor_copy(h_hi[:, j % 2, :], h[:, j % 2, :]).then_inc(h_hi_step, 1)
                v.wait_ge(h_hi_step, n + 1)
                v.tensor_tensor(h_lo[:, j % 2, :], h[:, j % 2, :], h_hi[:, j % 2, :].bitcast(F32), ALU.subtract).then_inc(h_split, 1)

            def result(k, q, b):
                v.wait_ge(down_done, 2 + MT * (k + 1))
                v.wait_ge(x1_biased, k + 1)
                for t in range(TT):
                    v.tensor_tensor(gated[:, t % 2, :], acc_bank[t][:, :], gate(b, G_MLP), ALU.mult).then_inc(acc_taken, 1)
                    v.wait_ge(acc_taken, 4 + TT * k + t + 1)
                    v.tensor_tensor(xb[:, q, t, :], xb[:, q, t, :], gated[:, t % 2, :], ALU.add).then_inc(out_ready, 1)

            def body(k, q, b, next_b, has_next):
                for j in range(MT):
                    n = MT * k + j
                    split_h(n, j)
                    if has_next or j < MT - 2:
                        high_w1(n + 2, (j + 2) % MT)
                    if has_next or j < MT - 1:
                        high_w2(n + 1, (j + 1) % MT)
                    if has_next:
                        if j == 1:
                            split_y(k + 1)
                        if 3 <= j < 3 + TT:
                            residual(k + 1, 1 - q, next_b, j - 3)
                        if j == 7:
                            variance(k + 1)
                        if j == 8:
                            normalise(k + 1, 1 - q)
                if has_next:
                    split_xm(k + 1)
                result(k, q, b)

            v.wait_ge(wo_in, 16)
            v.tensor_copy(wo_hi[:, :, :], xn[:, :, :]).then_inc(wo_hi_ready, 1)
            v.wait_ge(wo_hi_ready, 1)
            v.tensor_tensor(wo_lo[:, :, :], xn[:, :, :], wo_hi[:, :, :].bitcast(F32), ALU.subtract).then_inc(wo_split, 1)
            split_y(0)
            for t in range(TT):
                residual(0, 0, 0, t)
            variance(0)
            v.wait_ge(wo_split, 1)
            normalise(0, 0)
            v.wait_ge(w1_in, 16 * KT)
            high_w1(0, 0)
            high_w1(1, 1)
            v.wait_ge(w2_in, 16 * 4)
            high_w2(0, 0)
            split_xm(0)
            with v.Fori(0, NBLK // 2 - 1) as i:
                for q in range(2):
                    k = 2 * i + q
                    body(k, q, k // BPB, (k + 1) // BPB, True)
            body(NBLK - 2, 0, B - 1, B - 1, True)
            body(NBLK - 1, 1, B - 1, B - 1, False)

        @block.scalar
        def _(act):
            def bias_y(k):
                act.wait_ge(y_in, 16 * (k + 1))
                for g in range(G):
                    act.activation(yb[:, g, :], yb[:, g, :], ACT.Identity, bias=sh.vecs[:, ROW_BV + g:ROW_BV + g + 1]).then_inc(y_biased, 1)

            def modulate(k, b, t):
                act.wait_ge(t_done, KT * k + t + 1)
                act.wait_ge(xm_split, KT * k + t + 1)
                act.activation(xm[:, t, :], t_bank[:, :], ACT.Identity,
                               scale=sh.mod[:, bass.ds(b, 1), SCALE_MLP + t].rearrange("p a -> p (a)"),
                               bias=sh.mod[:, bass.ds(b, 1), SHIFT_MLP + t].rearrange("p a -> p (a)")).then_inc(t_taken, 1)

            def gelu(n, j):
                act.wait_ge(up_done, 2 + n + 1)
                act.wait_ge(h_split, n + 1)
                act.activation(h[:, j % 2, :], up_bank[j % 2][:, :], ACT.Gelu, bias=sh.vecs[:, ROW_B1 + j:ROW_B1 + j + 1]).then_inc(up_taken, 1)

            def body(k, next_b, has_next):
                for j in range(MT):
                    gelu(MT * k + j, j)
                    if has_next and j == 0:
                        bias_y(k + 1)
                    if has_next and 10 <= j < 10 + KT:
                        modulate(k + 1, next_b, j - 10)

            bias_y(0)
            for t in range(KT):
                modulate(0, 0, t)
            with act.Fori(0, NBLK // 2 - 1) as i:
                for q in range(2):
                    body(2 * i + q, (2 * i + q + 1) // BPB, True)
            body(NBLK - 2, B - 1, True)
            body(NBLK - 1, 0, False)

        @block.tensor
        def _(pe):
            def three(bank, first, last, hi_l, lo_l, hi_r, lo_r):
                pe.matmul(bank, hi_l, hi_r, start=first, stop=False)
                pe.matmul(bank, hi_l, lo_r, start=False, stop=False)
                return pe.matmul(bank, lo_l, hi_r, start=False, stop=last)

            def project_out(k, t):
                if t == 0:
                    pe.wait_ge(y_split, G * (k + 1))
                pe.wait_ge(wo_taken, TT * k + t + 1)
                s = slice(t * P, (t + 1) * P)
                for g in range(G):
                    last = three(o_bank[:, :], g == 0, g == G - 1, y_hi[:, g, s], y_lo[:, g, s], wo_hi[:, g, :], wo_lo[:, g, :])
                last.then_inc(wo_done, 1)

            def transposes(k, t):
                if t == 0:
                    pe.wait_ge(xn_ready, k + 1)
                pe.wait_ge(t_taken, KT * k + t + 1)
                for s in range(TT):
                    last = pe.transpose(t_bank[:, s * P:(s + 1) * P], xn[:, s, t * P:(t + 1) * P], sh.ident[:, :])
                last.then_inc(t_done, 1)

            def up(k, j):
                n = MT * k + j
                pe.wait_ge(w1_split, n + 1)
                pe.wait_ge(up_taken, n + 1)
                for t in range(KT):
                    if j == 0:
                        pe.wait_ge(xm_split, 4 + KT * k + t + 1)
                    last = three(up_bank[j % 2][:, :], t == 0, t == KT - 1, w1_hi[:, j % 2, t, :], w1_lo[:, j % 2, t, :],
                                 xm_hi[:, t, :], xm_lo[:, t, :])
                last.then_inc(up_done, 1)

            def down(k, j):
                n = MT * k + j
                pe.wait_ge(w2_split, n + 1)
                pe.wait_ge(h_split, 2 + n + 1)
                for t in range(TT):
                    if j == 0:
                        pe.wait_ge(acc_taken, TT * k + t + 1)
                    s = slice(t * P, (t + 1) * P)
                    last = three(acc_bank[t][:, :], j == 0, j == MT - 1, h_hi[:, j % 2, s], h_lo[:, j % 2, s],
                                 w2_hi[:, j % 2, :], w2_lo[:, j % 2, :])
                last.then_inc(down_done, 1)

            def body(k, has_next):
                for j in range(MT):
                    up(k, j)
                    if j:
                        down(k, j - 1)
                    if has_next and 3 <= j < 3 + TT:
                        project_out(k + 1, j - 3)
                    if has_next and 10 <= j < 10 + KT:
                        transposes(k + 1, j - 10)
                down(k, MT - 1)

            pe.wait_ge(wo_split, 1)
            for t in range(TT):
                project_out(0, t)
            for t in range(KT):
                transposes(0, t)
            with pe.Fori(0, NBLK // 2 - 1) as i:
                for q in range(2):
                    body(2 * i + q, True)
            body(NBLK - 2, True)
            body(NBLK - 1, False)


def program(nc, x, cond, Wc, bc, Wq, bq, Wk, bk, Wv, bv, Wo, bo, W1, b1, W2, b2, out):
    with ExitStack() as ctx:
        sh = Shared(nc, ctx)
        project(nc, sh, x, cond, Wc, bc, Wq, bq, Wk, bk, Wv, bv, b1, bo, b2)
        attend(nc, sh)
        feed_forward(nc, sh, x, Wo, W1, W2, out)


_INS = ["x", "cond_1024"] + ["L0_cond_" + n for n in "Wc bc Wq bq Wk bk Wv bv Wo bo W1 b1 W2 b2".split()]


def kernel(**inputs):
    import numpy as np
    import concourse.bacc as bacc
    from concourse.bass_utils import run_bass_kernel_spmd

    nc = bacc.Bacc("TRN2", target_bir_lowering=False, num_devices=1)
    arrays, args = {}, []
    for name in _INS:
        a = np.ascontiguousarray(inputs[name])
        arrays[f"in_{name}"] = a
        args.append(nc.dram_tensor(f"in_{name}", a.shape, mybir.dt.from_np(a.dtype), kind="ExternalInput").ap())
    out = nc.dram_tensor("out", (B, S, H), F32, kind="ExternalOutput").ap()
    program(nc, *args, out)
    r = run_bass_kernel_spmd(nc, [arrays], core_ids=[0])
    return r.results[0]["out"]
```

```python
import concourse.bass as bass
from concourse import mybir
from contextlib import ExitStack

F32 = mybir.dt.float32
F32R = mybir.dt.float32r
ALU = mybir.AluOpType
ACT = mybir.ActivationFunctionType
AX = mybir.AxisListType

P = 128
B, S, H = 2, 2048, 512
NH = 16
DH = H // NH
MLP = 4 * H
EPS = 1e-5
KT = H // P
HPG = P // DH
G = NH // HPG
TOK = 512
TT = TOK // P
NBLK = B * S // TOK
BPB = S // TOK
NKT = S // P
MT = MLP // P

ROW_BC, ROW_BQ, ROW_BK, ROW_BV, ROW_B1, ROW_C = 0, 6 * KT, 7 * KT, 8 * KT, 9 * KT, 9 * KT + MT
ROWS = ROW_C + B * KT
SCALE_MSA, SHIFT_MSA, SCALE_MLP, SHIFT_MLP = 0, KT, 2 * KT, 3 * KT
G_MSA, GBO, G_MLP, GB2 = range(4)


class Shared:

    def __init__(self, nc, ctx):
        def sb(name, shape):
            return ctx.enter_context(nc.sbuf_tensor(name, shape, F32))

        self.ident = sb("ident", [P, P])
        self.ones = sb("ones", [P, P])
        self.vecs = sb("vecs", [P, ROWS])
        self.bq_scaled = sb("bq_scaled", [P, KT])
        self.mod = sb("mod", [P, B, 4 * KT])
        self.gates = sb("gates", [P, B, 4, H])
        self.q_parts = nc.dram_tensor("q_parts", [B * G, P, 2, S], F32, kind="Internal").ap()
        self.k_parts = nc.dram_tensor("k_parts", [B * G, P, 2, S], F32, kind="Internal").ap()
        self.v_rows = nc.dram_tensor("v_rows", [B * S, H], F32, kind="Internal").ap()
        self.y_cols = nc.dram_tensor("y_cols", [B * G, P, S], F32, kind="Internal").ap()


def project(nc, sh, x, c, Wc, bc, Wq, bq, Wk, bk, Wv, bv, b1, bo, b2):
    with ExitStack() as ctx:
        def sb(name, shape, dt=F32):
            return ctx.enter_context(nc.sbuf_tensor(name, shape, dt))

        def pb(name, shape):
            return ctx.enter_context(nc.psum_tensor(name, shape, F32))

        def sem(name):
            return ctx.enter_context(nc.semaphore(name))

        rows = sb("rows", [ROWS, P])
        c_silu = sb("c_silu", [P, B * KT])
        c_wide = sb("c_wide", [P, B * KT, P])
        w_raw = sb("w_raw", [P, 2, KT, H])
        w_hi = sb("w_hi", [P, 3, KT, H], F32R)
        w_lo = sb("w_lo", [P, 3, KT, H], F32R)
        wc = sb("wc", [P, 4, KT, H])
        bc_wide = sb("bc_wide", [P, 4, H])
        xb = sb("xb", [P, 2, TT, H])
        stats = sb("stats", [P, TT, 6])
        mv = sb("mv", [P, TT, 2])
        var_eps = sb("var_eps", [P, TT])
        rstd = sb("rstd", [P, TT])
        neg_half = sb("neg_half", [P, TT])
        xm = sb("xm", [P, 2, TOK])
        xm_hi = sb("xm_hi", [P, 2, KT, TOK], F32R)
        xm_lo = sb("xm_lo", [P, 2, KT, TOK], F32R)
        qk = sb("qk", [P, 2, TOK])
        qk_out = sb("qk_out", [P, 4, 2, TOK], F32R)
        v_out = sb("v_out", [P, 2, H])

        mm_bank = [pb(f"mm_bank{n}", [P, TOK]) for n in range(4)]
        t_bank = [pb(f"t_bank{n}", [P, TOK]) for n in range(2)]
        c_bank = pb("c_bank", [P, H])
        g_bank = pb("g_bank", [P, H])

        rows_in, w_in, wide_in = sem("rows_in"), [sem(f"w_in{n}") for n in range(3)], sem("wide_in")
        wc_in = [sem(f"wc_in{n}") for n in range(6)]
        x_in = [sem(f"x_in{n}") for n in range(2)]
        const_ready, rows_t, vecs_ready = sem("const_ready"), sem("rows_t"), sem("vecs_ready")
        silu_ready, wide_ready = sem("silu_ready"), sem("wide_ready")
        c_done, c_taken, g_done, g_taken = sem("c_done"), sem("c_taken"), sem("g_done"), sem("g_taken")
        w_split = sem("w_split")
        stats_ready, rstd_ready, xn_ready = sem("stats_ready"), sem("rstd_ready"), sem("xn_ready")
        t_done, t_taken, xm_split = sem("t_done"), sem("t_taken"), sem("xm_split")
        mm_done, mm_taken, qk_split = sem("mm_done"), sem("mm_taken"), sem("qk_split")
        qk_stored = [sem(f"qk_stored{n}") for n in range(4)]
        v_stored = [sem(f"v_stored{n}") for n in range(2)]
        dve = sem("dve")
        norm_step, stats_seen, hi_step, qk_hi_step = sem("norm_step"), sem("stats_seen"), sem("hi_step"), sem("qk_hi_step")

        x_blocks = x.rearrange("b (n t p) d -> (b n) p t d", t=TT, p=P)
        v_blocks = sh.v_rows.rearrange("(n t p) d -> n t p d", t=TT, p=P)
        wc_parts = Wc.rearrange("(t p) (c n) -> c p t n", p=P, n=H)
        PER_BLOCK = 2 * G + TT
        N_QK = 2 * G
        block = ctx.enter_context(nc.Block())

        @block.sync
        def _(sp):
            for r, v, n in ((ROW_BC, bc, 6 * KT), (ROW_BQ, bq, KT), (ROW_BK, bk, KT), (ROW_BV, bv, KT), (ROW_B1, b1, MT)):
                sp.dma_start(rows[r:r + n, :], v.rearrange("(r p) -> r p", p=P)).then_inc(rows_in, 16)
            sp.dma_start(rows[ROW_C:ROWS, :], c.rearrange("b (t p) -> (b t) p", p=P)).then_inc(rows_in, 16)
            sp.dma_start(xb[:, 0, :, :], x_blocks[0]).then_inc(x_in[0], 16)
            for part in range(2):
                sp.dma_start(wc[:, part, :, :], wc_parts[part]).then_inc(wc_in[part], 16)
            for n, w in enumerate((Wq, Wk)):
                sp.dma_start(w_raw[:, n, :, :], w.rearrange("(t p) n -> p t n", p=P)).then_inc(w_in[n], 16)
            sp.dma_start(xb[:, 1, :, :], x_blocks[1]).then_inc(x_in[1], 16)
            for part in (2, 3):
                sp.dma_start(wc[:, part, :, :], wc_parts[part]).then_inc(wc_in[part], 16)
            for n, v in enumerate((bc[2 * H:3 * H], bc[5 * H:6 * H], bo, b2)):
                sp.dma_start(bc_wide[:, n, :], v.rearrange("(a n) -> a n", a=1).broadcast_to([P, H])).then_inc(wide_in, 16)
            sp.wait_ge(c_done, 2)
            for part in (4, 5):
                sp.dma_start(wc[:, part - 4, :, :], wc_parts[part]).then_inc(wc_in[part], 16)
            sp.wait_ge(w_split, 1)
            sp.dma_start(w_raw[:, 0, :, :], Wv.rearrange("(t p) n -> p t n", p=P)).then_inc(w_in[2], 16)

            def store(k, i, q, load_next):
                for m in range(N_QK):
                    dst = (sh.q_parts, sh.k_parts)[m % 2]
                    group, tok = sp.snap(k // BPB * G + m // 2), sp.snap(k % BPB * TOK)
                    sp.wait_ge(qk_split, 2 + N_QK * k + m + 1)
                    sp.dma_start(dst[bass.ds(group, 1), :, :, bass.ds(tok, TOK)].rearrange("a p s n -> p (a s) n"),
                                 qk_out[:, m % 4, :, :].bitcast(F32)).then_inc(qk_stored[m % 4], 16)
                    if m == N_QK // 2 and load_next:
                        sp.wait_ge(t_done, KT * (k + 1) + 1)
                        sp.dma_start(xb[:, q, :, :], x_blocks[k + 2]).then_inc(x_in[q], 16)
                for t in range(TT):
                    sp.wait_ge(mm_taken, 4 + PER_BLOCK * k + N_QK + t + 1)
                    sp.dma_start(v_blocks[k, t], v_out[:, t % 2, :]).then_inc(v_stored[t % 2], 16)

            with sp.Fori(0, NBLK // 2 - 1) as i:
                for q in range(2):
                    store(2 * i + q, i, q, True)
            for q in range(2):
                store(NBLK - 2 + q, NBLK // 2 - 1, q, False)
            for s in qk_stored:
                sp.wait_ge(s, 1 + 16 * NBLK * N_QK // 4)
            for s in v_stored:
                sp.wait_ge(s, 1 + 16 * NBLK * TT // 2)

        @block.gpsimd
        def _(pool):
            for s, n in ((t_taken, 2), (xm_split, 2), (mm_taken, 4), (qk_split, 2), (mm_done, 1)):
                pool.sem_inc(s, n)
            for s in qk_stored + v_stored:
                pool.sem_inc(s, 1)
            pool.memset(sh.ones[:, :], 1.0).then_inc(const_ready, 1)
            pool.memset(neg_half[:, :], -0.5).then_inc(const_ready, 1)
            pool.memset(sh.ident[:, :], 0.0).then_inc(const_ready, 1)
            pool.wait_ge(const_ready, 3)
            pool.affine_select(out=sh.ident[:, :], in_=sh.ident[:, :], compare_op=ALU.not_equal, fill=1.0,
                               base=0, pattern=[[-1, P]], channel_multiplier=1).then_inc(const_ready, 1)

            def root(k):
                pool.wait_ge(stats_ready, k + 1)
                pool.tensor_tensor(rstd[:, :], var_eps[:, :], neg_half[:, :], ALU.pow).then_inc(rstd_ready, 1)

            root(0)
            with pool.Fori(1, NBLK) as k:
                root(k)

        @block.vector
        def _(v):
            steps = [0]

            def after(ins):
                steps[0] += 1
                ins.then_inc(dve, 1)
                v.wait_ge(dve, steps[0])

            def norm(k, i, q):
                v.wait_ge(x_in[q], 16 * i + 16)
                for t in range(TT):
                    last = v.bn_stats(stats[:, t, :], xb[:, q, t, :])
                last.then_inc(norm_step, 1)
                v.wait_ge(norm_step, 2 * k + 1)
                v.sem_inc(stats_seen, 1)
                for t in range(TT):
                    last = v.bn_aggr(mv[:, t, :], stats[:, t, :])
                last.then_inc(norm_step, 1)
                v.wait_ge(norm_step, 2 * k + 2)
                v.tensor_scalar(var_eps[:, :], mv[:, :, 1], EPS, None, ALU.add).then_inc(stats_ready, 1)
                v.wait_ge(rstd_ready, k + 1)
                for t in range(TT):
                    last = v.tensor_scalar(xb[:, q, t, :], xb[:, q, t, :], mv[:, t, 0:1], rstd[:, t:t + 1],
                                           ALU.subtract, ALU.mult)
                last.then_inc(xn_ready, 1)

            def split_xm(k, q):
                v.wait_ge(mm_done, PER_BLOCK * (k - 1) + 1) if not isinstance(k, int) or k > 1 else None
                for t in range(KT):
                    v.wait_ge(t_taken, 2 + KT * k + t + 1)
                    v.tensor_copy(xm_hi[:, q, t, :], xm[:, t % 2, :]).then_inc(hi_step, 1)
                    v.wait_ge(hi_step, KT * k + t + 1)
                    v.tensor_tensor(xm_lo[:, q, t, :], xm[:, t % 2, :], xm_hi[:, q, t, :].bitcast(F32),
                                    ALU.subtract).then_inc(xm_split, 1)

            def split_qk(k, ms):
                for m in ms:
                    v.wait_ge(mm_taken, 4 + PER_BLOCK * k + m + 1)
                    v.wait_ge(qk_stored[m % 4], 16 * (k * N_QK // 4 + m // 4) + 1)
                    v.tensor_copy(qk_out[:, m % 4, 0, :], qk[:, m % 2, :]).then_inc(qk_hi_step, 1)
                    v.wait_ge(qk_hi_step, N_QK * k + m + 1)
                    v.tensor_tensor(qk_out[:, m % 4, 1, :], qk[:, m % 2, :], qk_out[:, m % 4, 0, :].bitcast(F32),
                                    ALU.subtract).then_inc(qk_split, 1)

            v.wait_ge(rows_t, 1)
            after(v.tensor_copy(sh.vecs[:, :], c_bank[:, 0:ROWS]))
            v.tensor_scalar(sh.bq_scaled[:, :], sh.vecs[:, ROW_BQ:ROW_BQ + KT], 1.0 / DH, None, ALU.mult).then_inc(vecs_ready, 1)
            norm(0, 0, 0)

            def mod_columns(part, column, one):
                v.wait_ge(c_done, {0: 1, 1: 2, 3: 3, 4: 4}[part])
                for b in range(B):
                    last = v.tensor_tensor(sh.mod[:, b, column:column + KT], c_bank[:, :].rearrange("p (t b) -> p b t", t=H // 2)[:, b, 0:KT],
                                           sh.vecs[:, ROW_BC + part * KT:ROW_BC + (part + 1) * KT], ALU.add)
                if one:
                    after(last)
                    last = v.tensor_scalar(sh.mod[:, :, column:column + KT], sh.mod[:, :, column:column + KT], 1.0, None, ALU.add)
                last.then_inc(c_taken, 1)

            mod_columns(0, SHIFT_MSA, False)
            mod_columns(1, SCALE_MSA, True)
            split_xm(0, 0)
            for n in range(3):
                v.wait_ge(w_in[n], 16)
                after(v.tensor_copy(w_hi[:, n, :, :], w_raw[:, n % 2, :, :]))
                v.tensor_tensor(w_lo[:, n, :, :], w_raw[:, n % 2, :, :], w_hi[:, n, :, :].bitcast(F32), ALU.subtract).then_inc(w_split, 1)
            v.wait_ge(silu_ready, 1)
            for n in range(B * KT):
                last = v.tensor_scalar(c_wide[:, n, :], sh.ones[:, :], c_silu[:, n:n + 1], None, ALU.mult)
            last.then_inc(wide_ready, 1)

            def body(k, i, q, has_next):
                if has_next:
                    norm(k + 1, i + q, 1 - q)
                split_qk(k, range(N_QK // 2))
                if has_next:
                    split_xm(k + 1, 1 - q)
                split_qk(k, range(N_QK // 2, N_QK))

            with v.Fori(0, NBLK // 2 - 1) as i:
                for q in range(2):
                    body(2 * i + q, i, q, True)
            body(NBLK - 2, NBLK // 2 - 1, 0, True)
            body(NBLK - 1, NBLK // 2 - 1, 1, False)

            mod_columns(3, SHIFT_MLP, False)
            mod_columns(4, SCALE_MLP, True)
            v.wait_ge(wide_in, 16 * 4)
            n = 0
            for part, gate, bias, wide in ((2, G_MSA, GBO, 0), (5, G_MLP, GB2, 1)):
                for b in range(B):
                    n += 1
                    v.wait_ge(g_done, n)
                    after(v.tensor_tensor(sh.gates[:, b, gate, :], g_bank[:, :], bc_wide[:, wide, :], ALU.add))
                    v.tensor_tensor(sh.gates[:, b, bias, :], sh.gates[:, b, gate, :], bc_wide[:, 2 + wide, :], ALU.mult).then_inc(g_taken, 1)

        @block.scalar
        def _(act):
            act.wait_ge(vecs_ready, 1)
            act.activation(c_silu[:, :], sh.vecs[:, ROW_C:ROWS], ACT.Silu).then_inc(silu_ready, 1)

            def modulate(k, b, t0=0):
                for t in range(KT):
                    act.wait_ge(t_done, KT * k + t + 1)
                    act.wait_ge(xm_split, KT * k + t + 1)
                    act.activation(xm[:, t % 2, :], t_bank[t % 2][:, :], ACT.Identity,
                                   scale=sh.mod[:, bass.ds(b, 1), SCALE_MSA + t].rearrange("p a -> p (a)"),
                                   bias=sh.mod[:, bass.ds(b, 1), SHIFT_MSA + t].rearrange("p a -> p (a)")).then_inc(t_taken, 1)

            def take_qk(k, ms):
                for m in ms:
                    act.wait_ge(mm_done, 1 + PER_BLOCK * k + m + 1)
                    act.wait_ge(qk_split, N_QK * k + m + 1)
                    g = m // 2
                    if m % 2 == 0:
                        ins = act.activation(qk[:, 0, :], mm_bank[m % 4][:, :], ACT.Identity,
                                             scale=1.0 / DH, bias=sh.bq_scaled[:, g:g + 1])
                    else:
                        ins = act.activation(qk[:, 1, :], mm_bank[m % 4][:, :], ACT.Identity,
                                             bias=sh.vecs[:, ROW_BK + g:ROW_BK + g + 1])
                    ins.then_inc(mm_taken, 1)

            def body(k, next_b, has_next):
                take_qk(k, range(N_QK // 2))
                if has_next:
                    modulate(k + 1, next_b)
                take_qk(k, range(N_QK // 2, N_QK))
                for t in range(TT):
                    act.wait_ge(mm_done, 1 + PER_BLOCK * k + N_QK + t + 1)
                    act.wait_ge(v_stored[t % 2], 16 * (k * TT // 2 + t // 2) + 1)
                    act.activation(v_out[:, t % 2, :], mm_bank[(N_QK + t) % 4][:, :], ACT.Copy).then_inc(mm_taken, 1)

            act.wait_ge(c_taken, 2)
            modulate(0, 0)
            with act.Fori(0, NBLK // 2 - 1) as i:
                for q in range(2):
                    body(2 * i + q, (2 * i + q + 1) // BPB, True)
            body(NBLK - 2, B - 1, True)
            body(NBLK - 1, 0, False)

        @block.tensor
        def _(pe):
            pe.wait_ge(rows_in, 16 * 6)
            pe.wait_ge(const_ready, 4)
            pe.transpose(c_bank[:, 0:ROWS], rows[:, :], sh.ident[0:ROWS, 0:ROWS]).then_inc(rows_t, 1)

            def columns(part):
                pe.wait_ge(wc_in[part], 16)
                for t in range(KT):
                    for s in range(KT):
                        last = pe.matmul(c_bank[:, t * B:(t + 1) * B], wc[:, part % 4, s, t * P:(t + 1) * P],
                                         c_silu[:, :].rearrange("p (b s) -> p s b", s=KT)[:, s, :],
                                         start=(s == 0), stop=(s == KT - 1))
                last.then_inc(c_done, 1)

            def transposes(k, q):
                pe.wait_ge(xn_ready, k + 1)
                for t in range(KT):
                    pe.wait_ge(t_taken, KT * k + t + 1)
                    for s in range(TT):
                        last = pe.transpose(t_bank[t % 2][:, s * P:(s + 1) * P], xb[:, q, s, t * P:(t + 1) * P], sh.ident[:, :])
                    last.then_inc(t_done, 1)

            def three(bank, hi_l, lo_l, hi_r, lo_r):
                for t in range(KT):
                    pe.matmul(bank, hi_l(t), hi_r(t), start=(t == 0), stop=False)
                    pe.matmul(bank, hi_l(t), lo_r(t), start=False, stop=False)
                    last = pe.matmul(bank, lo_l(t), hi_r(t), start=False, stop=(t == KT - 1))
                last.then_inc(mm_done, 1)

            def products(k, q, ms):
                for m in ms:
                    pe.wait_ge(mm_taken, PER_BLOCK * k + m + 1)
                    bank = mm_bank[m % 4][:, :]
                    if m < N_QK:
                        n, g = m % 2, m // 2
                        three(bank, lambda t: w_hi[:, n, t, g * P:(g + 1) * P], lambda t: w_lo[:, n, t, g * P:(g + 1) * P],
                              lambda t: xm_hi[:, q, t, :], lambda t: xm_lo[:, q, t, :])
                    else:
                        s = m - N_QK
                        three(bank, lambda t: xm_hi[:, q, t, s * P:(s + 1) * P], lambda t: xm_lo[:, q, t, s * P:(s + 1) * P],
                              lambda t: w_hi[:, 2, t, :], lambda t: w_lo[:, 2, t, :])

            def body(k, q, has_next):
                pe.wait_ge(xm_split, 2 + KT * (k + 1))
                products(k, q, range(N_QK // 2))
                if has_next:
                    transposes(k + 1, 1 - q)
                products(k, q, range(N_QK // 2, PER_BLOCK))

            pe.wait_ge(silu_ready, 1)
            columns(0)
            pe.wait_ge(c_taken, 1)
            columns(1)
            transposes(0, 0)
            pe.wait_ge(w_split, 3)
            with pe.Fori(0, NBLK // 2 - 1) as i:
                for q in range(2):
                    body(2 * i + q, q, True)
            body(NBLK - 2, 0, True)
            body(NBLK - 1, 1, False)

            pe.wait_ge(c_taken, 2)
            columns(3)
            pe.wait_ge(c_taken, 3)
            columns(4)
            pe.wait_ge(wide_ready, 1)
            n = 0
            for part in (2, 5):
                pe.wait_ge(wc_in[part], 16)
                for b in range(B):
                    if n:
                        pe.wait_ge(g_taken, n)
                    n += 1
                    for s in range(KT):
                        last = pe.matmul(g_bank[:, :], c_wide[:, b * KT + s, :], wc[:, part % 4, s, :],
                                         start=(s == 0), stop=(s == KT - 1))
                    last.then_inc(g_done, 1)


STACK = 3 * DH
Q_PARTS, K_PARTS = (0, 0, 1), (0, 1, 0)
N_IT = B * G * BPB
N_MAX = BPB * HPG * TT
CHUNK = TOK // P
N_PAIR = NKT // 2


def attend(nc, sh):
    with ExitStack() as ctx:
        def sb(name, shape, dt=F32):
            return ctx.enter_context(nc.sbuf_tensor(name, shape, dt))

        def pb(name, shape):
            return ctx.enter_context(nc.psum_tensor(name, shape, F32))

        def sem(name):
            return ctx.enter_context(nc.semaphore(name))

        km = sb("km", [STACK, HPG, S], F32R)
        ks = sb("ks", [STACK + 1, HPG, S], F32R)
        qm = [sb(f"qm{u}", [STACK, HPG, TOK], F32R) for u in range(2)]
        qs = [sb(f"qs{u}", [STACK + 1, HPG, TOK], F32R) for u in range(2)]
        vs = sb("vs", [P, NKT, P])
        probs = sb("probs", [P, 4, HPG, TOK])
        pair_sum = sb("pair_sum", [P, 2, 2, HPG, TOK])
        part_max = sb("part_max", [P, 2, HPG * TT, BPB])
        neg_max = sb("neg_max", [P, HPG * TT])
        neg_max_row = sb("neg_max_row", [HPG * TT, P], F32R)
        y_raw = sb("y_raw", [P, 2, TOK])
        d_raw, inv = sb("d_raw", [P, TOK]), sb("inv", [P, TOK])
        y_out = sb("y_out", [P, 2, TOK])

        s_bank = [pb(f"s_bank{n}", [P, TOK]) for n in range(3)]
        y_bank = pb("y_bank", [P, TOK])
        d_bank = pb("d_bank", [P, TOK])
        m_bank = [pb(f"m_bank{n}", [P, TOK]) for n in range(3)]

        km_in = [sem(f"km_in{c}") for c in range(BPB)]
        ks_in = [sem(f"ks_in{c}") for c in range(BPB)]
        v_in = [sem(f"v_in{c}") for c in range(BPB)]
        qm_in = [sem(f"qm_in{u}") for u in range(2)]
        qs_in = [sem(f"qs_in{u}") for u in range(2)]
        row_in = [sem(f"row_in{u}") for u in range(2)]
        ones_row = sem("ones_row")
        s_done, p_done, av_done, pair_ready, d_done = sem("s_done"), sem("p_done"), sem("av_done"), sem("pair_ready"), sem("d_done")
        quad_low, quad_high = sem("quad_low"), sem("quad_high")
        y_taken, d_taken, y_normed, inv_ready = sem("y_taken"), sem("d_taken"), sem("y_normed"), sem("inv_ready")
        y_stored = [sem(f"y_stored{u}") for u in range(2)]
        m_done, m_taken, neg_ready = sem("m_done"), sem("m_taken"), sem("neg_ready")
        LEAD = 12
        N_QUAD, N_SC = N_PAIR // 2, HPG * NKT
        M_USES = N_MAX + 1
        BEFORE = 2

        def place(i, n):
            return n + (1 if n >= BEFORE or (isinstance(i, int) and i == 0) else 0)

        def place_transposed(i):
            return 0 if isinstance(i, int) and i == N_IT - 1 else BEFORE

        def max_done(i, n):
            return M_USES * i + place(i, n)

        def transposed_done(i):
            return M_USES * (i + 1) + place_transposed(i)

        TAKEN = 3

        def before(at):
            return 2 if at < 2 else 3

        by_head = "a (h c) n -> c (a h) n"
        block = ctx.enter_context(nc.Block())

        @block.sync
        def _(sp):
            def load_rows(dst, src, parts, group, part_tok, n, done):
                for r, part in enumerate(parts):
                    sp.dma_start(dst(r), src[bass.ds(group, 1), :, part, part_tok:part_tok + n].rearrange(by_head, c=DH)).then_inc(done, 16)

            def load_km(group, c):
                load_rows(lambda r: km[r * DH:(r + 1) * DH, :, c * TOK:(c + 1) * TOK].bitcast(F32), sh.k_parts, K_PARTS, group, c * TOK, TOK, km_in[c])

            def load_ks(group, c):
                load_rows(lambda r: ks[r * DH:(r + 1) * DH, :, c * TOK:(c + 1) * TOK].bitcast(F32), sh.k_parts, K_PARTS, group, c * TOK, TOK, ks_in[c])

            def load_v(group, c):
                row, col = sp.snap(group // G * S + c * TOK), sp.snap(group % G * P)
                sp.dma_start(vs[:, c * CHUNK:(c + 1) * CHUNK, :],
                             sh.v_rows[bass.ds(row, TOK), bass.ds(col, P)].rearrange("(t p) n -> p t n", p=P)).then_inc(v_in[c], 16)

            def load_qm(group, qt):
                u = qt % 2
                load_rows(lambda r: qm[u][r * DH:(r + 1) * DH, :, :].bitcast(F32), sh.q_parts, Q_PARTS, group, qt * TOK, TOK, qm_in[u])

            def load_qs(group, qt):
                u = qt % 2
                load_rows(lambda r: qs[u][r * DH:(r + 1) * DH, :, :].bitcast(F32), sh.q_parts, Q_PARTS, group, qt * TOK, TOK, qs_in[u])

            def load_row(u):
                sp.dma_start(qs[u][STACK:STACK + 1, :, :].rearrange("a h n -> a (h n)").bitcast(F32),
                             neg_max_row[:, :].bitcast(F32)).then_inc(row_in[u], 16)

            def iteration(group, qt, last_group):
                i = BPB * group + qt
                following = [(group + (qt + d) // BPB, (qt + d) % BPB) for d in (1, 2)]
                there = [not (last_group and qt + d >= BPB) for d in (1, 2)]
                if there[1]:
                    sp.wait_ge(m_done, max_done(i, N_MAX - 1))
                    load_qm(*following[1])
                if there[0]:
                    sp.wait_ge(s_done, 1 + N_SC * i)
                    load_qs(*following[0])
                for c in range(BPB - 1 if qt == BPB - 1 else BPB):
                    if qt == BPB - 2 and not last_group:
                        sp.wait_ge(m_done, max_done(i + 1, HPG * TT * (c + 1) - 1))
                        load_km(group + 1, c)
                    if qt == BPB - 1 and not last_group:
                        sp.wait_ge(s_done, 1 + N_SC * i + HPG * CHUNK * (c + 1))
                        load_ks(group + 1, c)
                        sp.wait_ge(av_done, 4 + NKT * i + CHUNK * (c + 1))
                        load_v(group + 1, c)
                if there[0]:
                    sp.wait_ge(m_taken, TAKEN + transposed_done(i + 1))
                    load_row((qt + 1) % 2)
                if qt == BPB - 1 and not last_group:
                    c = BPB - 1
                    sp.wait_ge(s_done, 1 + N_SC * (i + 1))
                    load_ks(group + 1, c)
                    sp.wait_ge(av_done, 4 + NKT * (i + 1))
                    load_v(group + 1, c)

            load_qm(0, 0)
            for c in range(BPB):
                load_km(0, c)
            load_qm(0, 1)
            load_qs(0, 0)
            for c in range(BPB):
                load_ks(0, c)
                load_v(0, c)
            sp.wait_ge(m_taken, TAKEN + transposed_done(0))
            load_row(0)
            with sp.Fori(0, B * G - 1) as group:
                for qt in range(BPB):
                    iteration(group, qt, False)
            for qt in range(BPB):
                iteration(B * G - 1, qt, True)
            for u in range(2):
                sp.wait_ge(y_stored[u], 1 + 16 * N_IT // 2)

        @block.gpsimd
        def _(pool):
            for s, n in ((s_done, 1), (p_done, 2), (av_done, 4), (pair_ready, 2), (d_done, 2), (y_taken, 1),
                         (d_taken, 1), (y_normed, 2), (m_taken, TAKEN), (y_stored[0], 1), (y_stored[1], 1)):
                pool.sem_inc(s, n)
            pool.memset(ks[STACK:STACK + 1, :, :].bitcast(F32), 1.0).then_inc(ones_row, 1)
            with pool.Fori(0, N_IT) as i:
                for j in range(N_PAIR):
                    q, half = j // 2, j % 2
                    if half == 0:
                        pool.wait_ge(d_done, N_QUAD * i + q + 1)
                    for r in range(2):
                        pool.wait_ge(p_done, 2 + N_SC * i + HPG * (2 * j + 1) + 2 * r + 2)
                        ins = pool.tensor_tensor(pair_sum[:, q % 2, half, 2 * r:2 * r + 2, :], probs[:, 2 * j % 4, 2 * r:2 * r + 2, :],
                                                 probs[:, (2 * j + 1) % 4, 2 * r:2 * r + 2, :], ALU.add)
                    ins.then_inc(pair_ready, 1)
                    if half == 1:
                        pool.wait_ge(pair_ready, 2 + N_PAIR * i + j + 1)
                        pool.tensor_tensor(pair_sum[:, q % 2, 0, 2:4, :], pair_sum[:, q % 2, 0, 2:4, :],
                                           pair_sum[:, q % 2, 1, 2:4, :], ALU.add).then_inc(quad_high, 1)

        @block.scalar
        def _(act):
            def take_y(i, u):
                act.wait_ge(av_done, 4 + NKT * (i + 1))
                act.wait_ge(y_normed, i + 1)
                act.activation(y_raw[:, u, :], y_bank[:, :], ACT.Copy).then_inc(y_taken, 1)

            def take_sums(i):
                act.wait_ge(d_done, 2 + N_QUAD * (i + 1))
                act.wait_ge(y_normed, 2 + i)
                act.activation(d_raw[:, :], d_bank[:, :], ACT.Copy).then_inc(d_taken, 1)

            def store_y(i, u):
                group, tok = act.snap(i // BPB), act.snap(i % BPB * TOK)
                act.wait_ge(y_normed, 2 + i + 1)
                act.dma_start(sh.y_cols[bass.ds(group, 1), :, bass.ds(tok, TOK)].rearrange("a p n -> p (a n)"),
                              y_out[:, u, :]).then_inc(y_stored[u], 16)

            def body(i, u, has_prev):
                for t in range(NKT):
                    for h in range(HPG):
                        act.wait_ge(s_done, 1 + N_SC * i + HPG * t + h + 1)
                        if h == 0:
                            act.wait_ge(av_done, NKT * i + t + 1)
                            act.wait_ge(pair_ready, N_PAIR * i + t // 2 + 1)
                        act.activation(probs[:, t % 4, h, :], s_bank[(HPG * t + h) % 3][:, :], ACT.Exp).then_inc(p_done, 1)
                    if t == 0 and has_prev:
                        take_y(i - 1, 1 - u)
                    if t == 4 and has_prev:
                        take_sums(i - 1)
                    if t == 12 and has_prev:
                        store_y(i - 1, 1 - u)

            body(0, 0, False)
            with act.Fori(0, N_IT // 2 - 2) as j:
                body(2 * j + 1, 1, True)
                body(2 * j + 2, 0, True)
            for i in range(N_IT - 3, N_IT):
                body(i, i % 2, True)
            take_y(N_IT - 1, 1)
            take_sums(N_IT - 1)
            store_y(N_IT - 1, 1)

        @block.vector
        def _(v):
            def maximum(i, u, n):
                c, hs = n // (HPG * TT), n % (HPG * TT)
                v.wait_ge(m_done, max_done(i, n))
                v.tensor_reduce(part_max[:, u, hs, c:c + 1], m_bank[place(i, n) % 3][:, :], AX.X, ALU.max).then_inc(m_taken, 1)

            def negative(i, u):
                v.wait_ge(m_taken, TAKEN + max_done(i, N_MAX - 1))
                v.tensor_reduce(neg_max[:, :], part_max[:, u, :, :], AX.X, ALU.max, negate=True).then_inc(neg_ready, 1)

            def as_row(i, row_before=None):
                v.wait_ge(m_done, transposed_done(i))
                if row_before is not None:
                    v.wait_ge(*row_before)
                v.tensor_copy(neg_max_row[:, :], m_bank[place_transposed(i) % 3][0:HPG * TT, 0:P]).then_inc(m_taken, 1)

            def quad(i, q):
                v.wait_ge(pair_ready, 2 + N_PAIR * i + 2 * q + 2)
                v.tensor_tensor(pair_sum[:, q % 2, 0, 0:2, :], pair_sum[:, q % 2, 0, 0:2, :],
                                pair_sum[:, q % 2, 1, 0:2, :], ALU.add).then_inc(quad_low, 1)

            QUAD_AT, INVERT_AT, NORMALISE_AT = (44, 60, 10, 28), (32, 36, 48, 52), 56
            QUARTER = TOK // 4

            def invert(i, n):
                if n == 0:
                    v.wait_ge(d_taken, 1 + i + 1)
                s = slice(n * QUARTER, (n + 1) * QUARTER)
                v.reciprocal(inv[:, s], d_raw[:, s]).then_inc(inv_ready, 1)

            def normalise(i, u):
                v.wait_ge(y_taken, 1 + i + 1)
                v.wait_ge(y_stored[u], 16 * (i // 2) + 1)
                v.wait_ge(inv_ready, 4 * (i + 1))
                v.tensor_tensor(y_out[:, u, :], y_raw[:, u, :], inv[:, :], ALU.mult).then_inc(y_normed, 1)

            def body(i, u, has_prev, ahead):
                after = {(1, QUAD_AT[0]): [lambda: quad(i, 0)], (1, QUAD_AT[1]): [lambda: quad(i, 1)], (2, QUAD_AT[2]): [lambda: quad(i, 2)]}
                if has_prev:
                    after[1, QUAD_AT[3]] = [lambda: quad(i - 1, 3)]
                    for n, at in enumerate(INVERT_AT):
                        after.setdefault((1, at), []).append(lambda n=n: invert(i - 1, n))
                    after.setdefault((1, NORMALISE_AT), []).append(lambda: normalise(i - 1, 1 - u))

                def step(d, n):
                    if d <= ahead:
                        maximum(i + d, (u + d) % 2, n)
                    for work in after.get((d, n), ()):
                        work()

                for n in range(LEAD, N_MAX):
                    step(1, n)
                if ahead >= 1:
                    negative(i + 1, 1 - u)
                if ahead >= 2:
                    for n in range(BEFORE):
                        step(2, n)
                if ahead >= 1:
                    as_row(i + 1, (row_in[u], 16 * (i // 2 + 1)))
                for n in range(BEFORE if ahead >= 2 else 0, LEAD):
                    step(2, n)

            for n in range(N_MAX):
                maximum(0, 0, n)
            negative(0, 0)
            for n in range(BEFORE):
                maximum(1, 1, n)
            as_row(0)
            for n in range(BEFORE, LEAD):
                maximum(1, 1, n)
            body(0, 0, False, 2)
            with v.Fori(0, N_IT // 2 - 2) as j:
                body(2 * j + 1, 1, True, 2)
                body(2 * j + 2, 0, True, 2)
            for i in range(N_IT - 3, N_IT):
                body(i, i % 2, True, min(2, N_IT - 1 - i))
            quad(N_IT - 1, 3)
            for n in range(4):
                invert(N_IT - 1, n)
            normalise(N_IT - 1, 1)

        @block.tensor
        def _(pe):
            def max_product(i, u, n):
                c, h, s = n // (HPG * TT), n // TT % HPG, n % TT
                if n == 0:
                    pe.wait_ge(qm_in[u], 16 * 3 * (i // 2 + 1))
                if n % (HPG * TT) == 0:
                    pe.wait_ge(km_in[c], 16 * 3 * (i // BPB + 1))
                pe.wait_ge(m_taken, TAKEN + max_done(i, n) - before(place(i, n)))
                pe.matmul(m_bank[place(i, n) % 3][:, :], qm[u][:, h, s * P:(s + 1) * P], km[:, h, c * TOK:(c + 1) * TOK],
                          start=True, stop=True).then_inc(m_done, 1)

            def max_transpose(i):
                pe.wait_ge(neg_ready, i + 1)
                pe.wait_ge(m_taken, TAKEN + transposed_done(i) - before(place_transposed(i)))
                pe.transpose(m_bank[place_transposed(i) % 3][0:HPG * TT, 0:P], neg_max[:, :], sh.ident[:, :]).then_inc(m_done, 1)

            def scores(i, u, t, h):
                if h == 0 and t % CHUNK == 0:
                    pe.wait_ge(ks_in[t // CHUNK], 16 * 3 * (i // BPB + 1))
                n = HPG * t + h
                pe.wait_ge(p_done, 2 + N_SC * i + n + 1 - (1 if n == 0 else 3))
                pe.matmul(s_bank[n % 3][:, :], ks[:, h, t * P:(t + 1) * P], qs[u][:, h, :], start=True, stop=True).then_inc(s_done, 1)

            def times_v(i, t):
                if t % CHUNK == 0:
                    pe.wait_ge(v_in[t // CHUNK], 16 * (i // BPB + 1))
                if t == 0:
                    pe.wait_ge(y_taken, i + 1)
                pe.wait_ge(p_done, 2 + N_SC * i + HPG * (t + 1))
                for h in range(HPG):
                    last = pe.matmul(y_bank[h * DH:(h + 1) * DH, :], vs[:, t, h * DH:(h + 1) * DH], probs[:, t % 4, h, :],
                                     start=(t == 0), stop=(t == NKT - 1))
                last.then_inc(av_done, 1)

            def sums(i, q):
                if q == 0:
                    pe.wait_ge(d_taken, i + 1)
                pe.wait_ge(quad_low, N_QUAD * i + q + 1)
                pe.wait_ge(quad_high, N_QUAD * i + q + 1)
                for h in range(HPG):
                    last = pe.matmul(d_bank[h * DH:(h + 1) * DH, :], sh.ones[:, 0:DH], pair_sum[:, q % 2, 0, h, :],
                                     start=(q == 0), stop=(q == N_QUAD - 1))
                last.then_inc(d_done, 1)

            LATE = 2

            def body(i, u, has_prev, ahead):
                pe.wait_ge(qs_in[u], 16 * 3 * (i // 2 + 1))
                pe.wait_ge(row_in[u], 16 * (i // 2 + 1))
                left = []
                if ahead >= 1:
                    left = [lambda n=n: max_product(i + 1, 1 - u, n) for n in range(LEAD, N_MAX)]
                if ahead >= 2:
                    left += [lambda n=n: max_product(i + 2, u, n) for n in range(BEFORE)]
                if ahead >= 1:
                    left += [lambda: None] * (BEFORE if ahead == 1 else 0) + [lambda: max_transpose(i + 1)]
                if ahead >= 2:
                    left += [lambda n=n: max_product(i + 2, u, n) for n in range(BEFORE, LEAD)]

                def some_more(n):
                    for step in left[:n]:
                        step()
                    del left[:n]

                for t in range(NKT):
                    for h in range(HPG):
                        scores(i, u, t, h)
                        some_more(1)
                    if t > 0:
                        times_v(i, t - 1)
                    elif has_prev:
                        times_v(i - 1, NKT - 1)
                    if t % 4 == 0:
                        q = t // 4 - LATE
                        if q >= 0:
                            sums(i, q)
                        elif has_prev:
                            sums(i - 1, N_QUAD + q)
                some_more(len(left))

            for n in range(N_MAX):
                max_product(0, 0, n)
            for n in range(BEFORE):
                max_product(1, 1, n)
            max_transpose(0)
            for n in range(BEFORE, LEAD):
                max_product(1, 1, n)
            pe.wait_ge(ones_row, 1)
            body(0, 0, False, 2)
            with pe.Fori(0, N_IT // 2 - 2) as j:
                body(2 * j + 1, 1, True, 2)
                body(2 * j + 2, 0, True, 2)
            for i in range(N_IT - 3, N_IT):
                body(i, i % 2, True, min(2, N_IT - 1 - i))
            times_v(N_IT - 1, NKT - 1)
            for q in range(N_QUAD - LATE, N_QUAD):
                sums(N_IT - 1, q)


def feed_forward(nc, sh, x, Wo, W1, W2, out):
    with ExitStack() as ctx:
        def sb(name, shape, dt=F32):
            return ctx.enter_context(nc.sbuf_tensor(name, shape, dt))

        def pb(name, shape):
            return ctx.enter_context(nc.psum_tensor(name, shape, F32))

        def sem(name):
            return ctx.enter_context(nc.semaphore(name))

        w1_raw = sb("w1_raw", [P, KT, MLP])
        w2_raw = sb("w2_raw", [P, MT, H])
        w1_hi, w1_lo = sb("w1_hi", [P, 2, KT, P], F32R), sb("w1_lo", [P, 2, KT, P], F32R)
        w2_hi, w2_lo = sb("w2_hi", [P, 2, H], F32R), sb("w2_lo", [P, 2, H], F32R)
        wo_hi, wo_lo = sb("wo_hi", [P, KT, H], F32R), sb("wo_lo", [P, KT, H], F32R)
        yb = sb("yb", [P, KT, TOK])
        y_hi, y_lo = sb("y_hi", [P, KT, TOK], F32R), sb("y_lo", [P, KT, TOK], F32R)
        xb = sb("xb2", [P, 2, TT, H])
        stats, mv = sb("stats2", [P, TT, 6]), sb("mv2", [P, TT, 2])
        var_eps, rstd, neg_half = sb("var_eps2", [P, TT]), sb("rstd2", [P, TT]), sb("neg_half2", [P, TT])
        xn = sb("xn", [P, TT, H])
        xm = sb("xm2", [P, KT, TOK])
        xm_hi, xm_lo = sb("xm2_hi", [P, KT, TOK], F32R), sb("xm2_lo", [P, KT, TOK], F32R)
        h = sb("h", [P, 2, TOK])
        h_hi, h_lo = sb("h_hi", [P, 2, TOK], F32R), sb("h_lo", [P, 2, TOK], F32R)
        gated = sb("gated", [P, 2, H])

        acc_bank = [pb(f"acc_bank{t}", [P, H]) for t in range(TT)]
        up_bank = [pb(f"up_bank{n}", [P, TOK]) for n in range(2)]
        o_bank = pb("o_bank", [P, H])
        t_bank = pb("t_bank", [P, TOK])

        wo_in, w1_in, w2_in, y_in = sem("wo_in"), sem("w1_in"), sem("w2_in"), sem("y_in")
        x_in = [sem(f"x2_in{q}") for q in range(2)]
        stored = [sem(f"stored{q}") for q in range(2)]
        wo_hi_ready, wo_split, half_ready = sem("wo_hi_ready"), sem("wo_split"), sem("half_ready")
        y_biased, y_split, y_hi_step = sem("y_biased"), sem("y_split"), sem("y_hi_step")
        x_biased, wo_done, wo_taken, gated_step, x1_step = sem("x_biased"), sem("wo_done"), sem("wo_taken"), sem("gated_step"), sem("x1_step")
        norm_step, stats_seen, stats_ready, rstd_ready, xn_ready, x1_biased = (
            sem("norm_step2"), sem("stats_seen2"), sem("stats_ready2"), sem("rstd_ready2"), sem("xn_ready2"), sem("x1_biased"))
        t_done, t_taken, xm_hi_step, xm_split = sem("t_done2"), sem("t_taken2"), sem("xm_hi_step"), sem("xm_split2")
        up_done, up_taken, h_hi_step, h_split, down_done = sem("up_done"), sem("up_taken"), sem("h_hi_step"), sem("h_split"), sem("down_done")
        w1_hi_ready, w1_split, w2_hi_ready, w2_split = sem("w1_hi_ready"), sem("w1_split"), sem("w2_hi_ready"), sem("w2_split")
        acc_taken, acc_step, out_ready = sem("acc_taken"), sem("acc_step"), sem("out_ready")

        x_blocks = x.rearrange("b (n t p) d -> (b n) p t d", t=TT, p=P)
        out_blocks = out.rearrange("b (n t p) d -> (b n) t p d", t=TT, p=P)
        block = ctx.enter_context(nc.Block())

        def gate(b, which):
            return sh.gates[:, bass.ds(b, 1), which, :].rearrange("p a n -> p (a n)")

        @block.sync
        def _(sp):
            def load_y(k):
                group, tok = sp.snap(k // BPB * G), sp.snap(k % BPB * TOK)
                sp.dma_start(yb[:, :, :], sh.y_cols[bass.ds(group, G), :, bass.ds(tok, TOK)].rearrange("g p n -> p g n")).then_inc(y_in, 16)

            sp.dma_start(xn[:, :, :], Wo.rearrange("(t p) n -> p t n", p=P)).then_inc(wo_in, 16)
            sp.dma_start(yb[:, :, :], sh.y_cols[0:G, :, 0:TOK].rearrange("g p n -> p g n")).then_inc(y_in, 16)
            sp.dma_start(xb[:, 0, :, :], x_blocks[0]).then_inc(x_in[0], 16)
            for t in range(KT):
                sp.dma_start(w1_raw[:, t, :], W1[t * P:(t + 1) * P, :]).then_inc(w1_in, 16)
            sp.dma_start(xb[:, 1, :, :], x_blocks[1]).then_inc(x_in[1], 16)
            for n in range(4):
                sp.dma_start(w2_raw[:, n * MT // 4:(n + 1) * MT // 4, :],
                             W2[n * MLP // 4:(n + 1) * MLP // 4, :].rearrange("(j p) n -> p j n", p=P)).then_inc(w2_in, 16)
            sp.wait_ge(y_split, KT)
            load_y(1)

            def body(k, i, q, load_next):
                if load_next:
                    sp.wait_ge(y_split, KT * (k + 2))
                    load_y(k + 2)
                for t in range(TT):
                    sp.wait_ge(out_ready, TT * k + t + 1)
                    sp.dma_start(out_blocks[k, t], xb[:, q, t, :]).then_inc(stored[q], 16)
                if load_next:
                    sp.wait_ge(stored[q], 16 * TT * (i + 1))
                    sp.dma_start(xb[:, q, :, :], x_blocks[k + 2]).then_inc(x_in[q], 16)

            with sp.Fori(0, NBLK // 2 - 1) as i:
                for q in range(2):
                    body(2 * i + q, i, q, True)
            for q in range(2):
                body(NBLK - 2 + q, NBLK // 2 - 1, q, False)
            for q in range(2):
                sp.wait_ge(stored[q], 16 * TT * NBLK // 2)

        @block.gpsimd
        def _(pool):
            for s, n in ((wo_done, 1), (wo_taken, 1), (t_taken, 1), (xm_split, 4), (up_done, 2), (up_taken, 2),
                         (h_split, 2), (down_done, 2), (acc_taken, 4)):
                pool.sem_inc(s, n)
            pool.memset(neg_half[:, :], -0.5).then_inc(half_ready, 1)
            pool.wait_ge(half_ready, 1)

            def bias_x(k, i, q, b):
                pool.wait_ge(x_in[q], 16 * (i + 1))
                for t in range(TT):
                    pool.tensor_tensor(xb[:, q, t, :], xb[:, q, t, :], gate(b, GBO), ALU.add).then_inc(x_biased, 1)

            def root(k):
                pool.wait_ge(stats_ready, k + 1)
                pool.tensor_tensor(rstd[:, :], var_eps[:, :], neg_half[:, :], ALU.pow).then_inc(rstd_ready, 1)

            def bias_x1(k, q, b):
                pool.wait_ge(xn_ready, k + 1)
                for t in range(TT):
                    ins = pool.tensor_tensor(xb[:, q, t, :], xb[:, q, t, :], gate(b, GB2), ALU.add)
                ins.then_inc(x1_biased, 1)

            def split_w1(n, j):
                pool.wait_ge(w1_hi_ready, n + 1)
                pool.tensor_tensor(w1_lo[:, j % 2, :, :], w1_raw[:, :, j * P:(j + 1) * P], w1_hi[:, j % 2, :, :].bitcast(F32),
                                   ALU.subtract).then_inc(w1_split, 1)

            def split_w2(n, j):
                pool.wait_ge(w2_hi_ready, n + 1)
                pool.tensor_tensor(w2_lo[:, j % 2, :], w2_raw[:, j, :], w2_hi[:, j % 2, :].bitcast(F32), ALU.subtract).then_inc(w2_split, 1)

            def body(k, i, q, b, has_next):
                for j in range(MT):
                    n = MT * k + j
                    if has_next or j < MT - 2:
                        split_w1(n + 2, (j + 2) % MT)
                    if has_next or j < MT - 1:
                        split_w2(n + 1, (j + 1) % MT)
                    if has_next:
                        if j == 0:
                            bias_x(k + 1, i, 1 - q, b)
                        if j == 8:
                            root(k + 1)
                        if j == 9:
                            bias_x1(k + 1, 1 - q, b)

            bias_x(0, 0, 0, 0)
            root(0)
            bias_x1(0, 0, 0)
            split_w1(0, 0)
            split_w1(1, 1)
            split_w2(0, 0)
            with pool.Fori(0, NBLK // 2 - 1) as i:
                for q in range(2):
                    body(2 * i + q, i + q, q, (2 * i + q + 1) // BPB, True)
            body(NBLK - 2, NBLK // 2 - 1, 0, B - 1, True)
            body(NBLK - 1, 0, 1, B - 1, False)

        @block.vector
        def _(v):
            def split_y(k):
                v.wait_ge(wo_done, TT * k + 1)
                for g in range(G):
                    v.wait_ge(y_biased, G * k + g + 1)
                    v.tensor_copy(y_hi[:, g, :], yb[:, g, :]).then_inc(y_hi_step, 1)
                    v.wait_ge(y_hi_step, G * k + g + 1)
                    v.tensor_tensor(y_lo[:, g, :], yb[:, g, :], y_hi[:, g, :].bitcast(F32), ALU.subtract).then_inc(y_split, 1)

            def residual(k, q, b, t):
                n = TT * k + t
                v.wait_ge(wo_done, 1 + n + 1)
                v.tensor_tensor(gated[:, t % 2, :], o_bank[:, :], gate(b, G_MSA), ALU.mult).then_inc(wo_taken, 1)
                v.wait_ge(wo_taken, 1 + n + 1)
                v.wait_ge(x_biased, n + 1)
                v.tensor_tensor(xb[:, q, t, :], xb[:, q, t, :], gated[:, t % 2, :], ALU.add).then_inc(x1_step, 1)
                v.wait_ge(x1_step, n + 1)
                v.bn_stats(stats[:, t, :], xb[:, q, t, :]).then_inc(norm_step, 1)

            def variance(k):
                v.wait_ge(norm_step, (TT + 1) * k + TT)
                v.sem_inc(stats_seen, 1)
                for t in range(TT):
                    last = v.bn_aggr(mv[:, t, :], stats[:, t, :])
                last.then_inc(norm_step, 1)
                v.wait_ge(norm_step, (TT + 1) * (k + 1))
                v.tensor_scalar(var_eps[:, :], mv[:, :, 1], EPS, None, ALU.add).then_inc(stats_ready, 1)

            def normalise(k, q):
                v.wait_ge(rstd_ready, k + 1)
                for t in range(TT):
                    last = v.tensor_scalar(xn[:, t, :], xb[:, q, t, :], mv[:, t, 0:1], rstd[:, t:t + 1], ALU.subtract, ALU.mult)
                last.then_inc(xn_ready, 1)

            def split_xm(k):
                v.wait_ge(up_done, MT * k + 2)
                for t in range(KT):
                    v.wait_ge(t_taken, 1 + KT * k + t + 1)
                    v.tensor_copy(xm_hi[:, t, :], xm[:, t, :]).then_inc(xm_hi_step, 1)
                    v.wait_ge(xm_hi_step, KT * k + t + 1)
                    v.tensor_tensor(xm_lo[:, t, :], xm[:, t, :], xm_hi[:, t, :].bitcast(F32), ALU.subtract).then_inc(xm_split, 1)

            def high_w1(n, j):
                v.wait_ge(up_done, n + 1)
                v.tensor_copy(w1_hi[:, j % 2, :, :], w1_raw[:, :, j * P:(j + 1) * P]).then_inc(w1_hi_ready, 1)

            def high_w2(n, j):
                v.wait_ge(down_done, n + 1)
                v.tensor_copy(w2_hi[:, j % 2, :], w2_raw[:, j, :]).then_inc(w2_hi_ready, 1)

            def split_h(n, j):
                v.wait_ge(up_taken, 2 + n + 1)
                v.wait_ge(down_done, n + 1)
                v.tensor_copy(h_hi[:, j % 2, :], h[:, j % 2, :]).then_inc(h_hi_step, 1)
                v.wait_ge(h_hi_step, n + 1)
                v.tensor_tensor(h_lo[:, j % 2, :], h[:, j % 2, :], h_hi[:, j % 2, :].bitcast(F32), ALU.subtract).then_inc(h_split, 1)

            def result(k, q, b):
                v.wait_ge(down_done, 2 + MT * (k + 1))
                v.wait_ge(x1_biased, k + 1)
                for t in range(TT):
                    v.tensor_tensor(gated[:, t % 2, :], acc_bank[t][:, :], gate(b, G_MLP), ALU.mult).then_inc(acc_taken, 1)
                    v.wait_ge(acc_taken, 4 + TT * k + t + 1)
                    v.tensor_tensor(xb[:, q, t, :], xb[:, q, t, :], gated[:, t % 2, :], ALU.add).then_inc(out_ready, 1)

            def body(k, q, b, next_b, has_next):
                for j in range(MT):
                    n = MT * k + j
                    split_h(n, j)
                    if has_next or j < MT - 2:
                        high_w1(n + 2, (j + 2) % MT)
                    if has_next or j < MT - 1:
                        high_w2(n + 1, (j + 1) % MT)
                    if has_next:
                        if j == 1:
                            split_y(k + 1)
                        if 3 <= j < 3 + TT:
                            residual(k + 1, 1 - q, next_b, j - 3)
                        if j == 7:
                            variance(k + 1)
                        if j == 8:
                            normalise(k + 1, 1 - q)
                if has_next:
                    split_xm(k + 1)
                result(k, q, b)

            v.wait_ge(wo_in, 16)
            v.tensor_copy(wo_hi[:, :, :], xn[:, :, :]).then_inc(wo_hi_ready, 1)
            v.wait_ge(wo_hi_ready, 1)
            v.tensor_tensor(wo_lo[:, :, :], xn[:, :, :], wo_hi[:, :, :].bitcast(F32), ALU.subtract).then_inc(wo_split, 1)
            split_y(0)
            for t in range(TT):
                residual(0, 0, 0, t)
            variance(0)
            v.wait_ge(wo_split, 1)
            normalise(0, 0)
            v.wait_ge(w1_in, 16 * KT)
            high_w1(0, 0)
            high_w1(1, 1)
            v.wait_ge(w2_in, 16 * 4)
            high_w2(0, 0)
            split_xm(0)
            with v.Fori(0, NBLK // 2 - 1) as i:
                for q in range(2):
                    k = 2 * i + q
                    body(k, q, k // BPB, (k + 1) // BPB, True)
            body(NBLK - 2, 0, B - 1, B - 1, True)
            body(NBLK - 1, 1, B - 1, B - 1, False)

        @block.scalar
        def _(act):
            def bias_y(k):
                act.wait_ge(y_in, 16 * (k + 1))
                for g in range(G):
                    act.activation(yb[:, g, :], yb[:, g, :], ACT.Identity, bias=sh.vecs[:, ROW_BV + g:ROW_BV + g + 1]).then_inc(y_biased, 1)

            def modulate(k, b, t):
                act.wait_ge(t_done, KT * k + t + 1)
                act.wait_ge(xm_split, KT * k + t + 1)
                act.activation(xm[:, t, :], t_bank[:, :], ACT.Identity,
                               scale=sh.mod[:, bass.ds(b, 1), SCALE_MLP + t].rearrange("p a -> p (a)"),
                               bias=sh.mod[:, bass.ds(b, 1), SHIFT_MLP + t].rearrange("p a -> p (a)")).then_inc(t_taken, 1)

            def gelu(n, j):
                act.wait_ge(up_done, 2 + n + 1)
                act.wait_ge(h_split, n + 1)
                act.activation(h[:, j % 2, :], up_bank[j % 2][:, :], ACT.Gelu, bias=sh.vecs[:, ROW_B1 + j:ROW_B1 + j + 1]).then_inc(up_taken, 1)

            def body(k, next_b, has_next):
                for j in range(MT):
                    gelu(MT * k + j, j)
                    if has_next and j == 0:
                        bias_y(k + 1)
                    if has_next and 10 <= j < 10 + KT:
                        modulate(k + 1, next_b, j - 10)

            bias_y(0)
            for t in range(KT):
                modulate(0, 0, t)
            with act.Fori(0, NBLK // 2 - 1) as i:
                for q in range(2):
                    body(2 * i + q, (2 * i + q + 1) // BPB, True)
            body(NBLK - 2, B - 1, True)
            body(NBLK - 1, 0, False)

        @block.tensor
        def _(pe):
            def three(bank, first, last, hi_l, lo_l, hi_r, lo_r):
                pe.matmul(bank, hi_l, hi_r, start=first, stop=False)
                pe.matmul(bank, hi_l, lo_r, start=False, stop=False)
                return pe.matmul(bank, lo_l, hi_r, start=False, stop=last)

            def project_out(k, t):
                if t == 0:
                    pe.wait_ge(y_split, G * (k + 1))
                pe.wait_ge(wo_taken, TT * k + t + 1)
                s = slice(t * P, (t + 1) * P)
                for g in range(G):
                    last = three(o_bank[:, :], g == 0, g == G - 1, y_hi[:, g, s], y_lo[:, g, s], wo_hi[:, g, :], wo_lo[:, g, :])
                last.then_inc(wo_done, 1)

            def transposes(k, t):
                if t == 0:
                    pe.wait_ge(xn_ready, k + 1)
                pe.wait_ge(t_taken, KT * k + t + 1)
                for s in range(TT):
                    last = pe.transpose(t_bank[:, s * P:(s + 1) * P], xn[:, s, t * P:(t + 1) * P], sh.ident[:, :])
                last.then_inc(t_done, 1)

            def up(k, j):
                n = MT * k + j
                pe.wait_ge(w1_split, n + 1)
                pe.wait_ge(up_taken, n + 1)
                for t in range(KT):
                    if j == 0:
                        pe.wait_ge(xm_split, 4 + KT * k + t + 1)
                    last = three(up_bank[j % 2][:, :], t == 0, t == KT - 1, w1_hi[:, j % 2, t, :], w1_lo[:, j % 2, t, :],
                                 xm_hi[:, t, :], xm_lo[:, t, :])
                last.then_inc(up_done, 1)

            def down(k, j):
                n = MT * k + j
                pe.wait_ge(w2_split, n + 1)
                pe.wait_ge(h_split, 2 + n + 1)
                for t in range(TT):
                    if j == 0:
                        pe.wait_ge(acc_taken, TT * k + t + 1)
                    s = slice(t * P, (t + 1) * P)
                    last = three(acc_bank[t][:, :], j == 0, j == MT - 1, h_hi[:, j % 2, s], h_lo[:, j % 2, s],
                                 w2_hi[:, j % 2, :], w2_lo[:, j % 2, :])
                last.then_inc(down_done, 1)

            def body(k, has_next):
                for j in range(MT):
                    up(k, j)
                    if j:
                        down(k, j - 1)
                    if has_next and 3 <= j < 3 + TT:
                        project_out(k + 1, j - 3)
                    if has_next and 10 <= j < 10 + KT:
                        transposes(k + 1, j - 10)
                down(k, MT - 1)

            pe.wait_ge(wo_split, 1)
            for t in range(TT):
                project_out(0, t)
            for t in range(KT):
                transposes(0, t)
            with pe.Fori(0, NBLK // 2 - 1) as i:
                for q in range(2):
                    body(2 * i + q, True)
            body(NBLK - 2, True)
            body(NBLK - 1, False)


def program(nc, x, cond, Wc, bc, Wq, bq, Wk, bk, Wv, bv, Wo, bo, W1, b1, W2, b2, out):
    with ExitStack() as ctx:
        sh = Shared(nc, ctx)
        project(nc, sh, x, cond, Wc, bc, Wq, bq, Wk, bk, Wv, bv, b1, bo, b2)
        attend(nc, sh)
        feed_forward(nc, sh, x, Wo, W1, W2, out)


_INS = ["x", "cond_1024"] + ["L0_cond_" + n for n in "Wc bc Wq bq Wk bk Wv bv Wo bo W1 b1 W2 b2".split()]


def kernel(**inputs):
    import numpy as np
    import concourse.bacc as bacc
    from concourse.bass_utils import run_bass_kernel_spmd

    nc = bacc.Bacc("TRN2", target_bir_lowering=False, num_devices=1)
    arrays, args = {}, []
    for name in _INS:
        a = np.ascontiguousarray(inputs[name])
        arrays[f"in_{name}"] = a
        args.append(nc.dram_tensor(f"in_{name}", a.shape, mybir.dt.from_np(a.dtype), kind="ExternalInput").ap())
    out = nc.dram_tensor("out", (B, S, H), F32, kind="ExternalOutput").ap()
    program(nc, *args, out)
    r = run_bass_kernel_spmd(nc, [arrays], core_ids=[0])
    return r.results[0]["out"]
```

```python
import concourse.bass as bass
from concourse import mybir
from contextlib import ExitStack

F32 = mybir.dt.float32
F32R = mybir.dt.float32r
ALU = mybir.AluOpType
ACT = mybir.ActivationFunctionType
AX = mybir.AxisListType

P = 128
B, S, H = 2, 2048, 512
NH = 16
DH = H // NH
MLP = 4 * H
EPS = 1e-5
KT = H // P
HPG = P // DH
G = NH // HPG
TOK = 512
TT = TOK // P
NBLK = B * S // TOK
BPB = S // TOK
NKT = S // P
MT = MLP // P

ROW_BC, ROW_BQ, ROW_BK, ROW_BV, ROW_B1, ROW_C = 0, 6 * KT, 7 * KT, 8 * KT, 9 * KT, 9 * KT + MT
ROWS = ROW_C + B * KT
SCALE_MSA, SHIFT_MSA, SCALE_MLP, SHIFT_MLP = 0, KT, 2 * KT, 3 * KT
G_MSA, GBO, G_MLP, GB2 = range(4)


class Space:

    def __init__(self, nc, ctx, name):
        self.parts = ctx.enter_context(nc.sbuf_tensor(f"{name}_parts", [P, KT, TOK], F32R))
        size = KT * TOK * 4
        self.plain = nc.alloc_sbuf_tensor_at(f"{name}_plain", [P, KT, TOK], F32, offset=nc.sbuf_base - size)


class Shared:

    def __init__(self, nc, ctx):
        def sb(name, shape):
            return ctx.enter_context(nc.sbuf_tensor(name, shape, F32))

        self.ident = sb("ident", [P, P])
        self.ones = sb("ones", [P, P])
        self.vecs = sb("vecs", [P, ROWS])
        self.bq_scaled = sb("bq_scaled", [P, KT])
        self.mod = sb("mod", [P, B, 4 * KT])
        self.gates = sb("gates", [P, B, 4, H])
        self.space = [Space(nc, ctx, f"space{n}") for n in range(3)]
        self.q_parts = nc.dram_tensor("q_parts", [B * G, P, 2, S], F32, kind="Internal").ap()
        self.k_parts = nc.dram_tensor("k_parts", [B * G, P, 2, S], F32, kind="Internal").ap()
        self.v_rows = nc.dram_tensor("v_rows", [B * S, H], F32, kind="Internal").ap()
        self.inv_rows = nc.dram_tensor("inv_rows", [HPG, TOK], F32, kind="Internal").ap()
        self.y_cols = nc.dram_tensor("y_cols", [B * G, P, S], F32, kind="Internal").ap()


class Late:

    def __init__(self, nc, ctx):
        self.space = [Space(nc, ctx, f"late{n}") for n in range(3)]
        self.wo = ctx.enter_context(nc.sbuf_tensor("wo", [P, KT, H], F32))


def load_stacked(sp, dst, src, parts, group, tok, done):
    for r, part in enumerate(parts):
        sp.dma_start(dst[r * DH:(r + 1) * DH, :, :].bitcast(F32),
                     src[bass.ds(group, 1), :, part, tok:tok + TOK].rearrange("a (h c) n -> c (a h) n", c=DH)).then_inc(done, 16)


def project(nc, sh, x, c, Wc, bc, Wq, bq, Wk, bk, Wv, bv, b1, bo, b2):
    with ExitStack() as ctx:
        def sb(name, shape, dt=F32):
            return ctx.enter_context(nc.sbuf_tensor(name, shape, dt))

        def pb(name, shape):
            return ctx.enter_context(nc.psum_tensor(name, shape, F32))

        def sem(name):
            return ctx.enter_context(nc.semaphore(name))

        rows = sb("rows", [ROWS, P])
        c_silu = sb("c_silu", [P, KT, P // KT])
        select = sb("select", [P, B])
        select_wide = sb("select_wide", [P, B, P])
        c_part = sb("c_part", [P, 2, H])
        w_raw = [t.plain[:, :, :] for t in sh.space]
        w_hi = sb("w_hi", [P, 3, KT, H], F32R)
        w_lo = sb("w_lo", [P, 3, KT, H], F32R)
        wc = sb("wc", [P, 2, KT, H])
        bc_wide = sb("bc_wide", [P, 4, H])
        xb = sb("xb", [P, 2, TT, H])
        stats = sb("stats", [P, TT, 6])
        mv = sb("mv", [P, TT, 2])
        var_eps = sb("var_eps", [P, TT])
        rstd = sb("rstd", [P, TT])
        neg_half = sb("neg_half", [P, TT])
        xm = sb("xm", [P, 2, TOK])
        xm_hi = sb("xm_hi", [P, 2, KT, TOK], F32R)
        xm_lo = sb("xm_lo", [P, 2, KT, TOK], F32R)
        qk = sb("qk", [P, 2, TOK])
        qk_out = sb("qk_out", [P, 4, 2, TOK], F32R)
        v_out = sb("v_out", [P, 2, H])

        mm_bank = [pb(f"mm_bank{n}", [P, TOK]) for n in range(4)]
        t_bank = [pb(f"t_bank{n}", [P, TOK]) for n in range(2)]
        c_bank = pb("c_bank", [P, H])
        g_bank = pb("g_bank", [P, H])

        rows_in, w_in, wide_in = sem("rows_in"), [sem(f"w_in{n}") for n in range(3)], sem("wide_in")
        wc_in = [sem(f"wc_in{n}") for n in range(6)]
        x_in = [sem(f"x_in{n}") for n in range(2)]
        const_ready, rows_t, vecs_ready = sem("const_ready"), sem("rows_t"), sem("vecs_ready")
        next_in = sem("next_in")
        silu_ready, select_ready = sem("silu_ready"), sem("select_ready")
        c_done, c_taken, g_done, g_taken = sem("c_done"), sem("c_taken"), sem("g_done"), sem("g_taken")
        w_hi_ready, w_split = sem("w_hi_ready"), [sem(f"w_split{n}") for n in range(3)]
        stats_ready, rstd_ready, xn_ready = sem("stats_ready"), sem("rstd_ready"), sem("xn_ready")
        t_done, t_taken, xm_split = sem("t_done"), sem("t_taken"), sem("xm_split")
        mm_done, mm_taken, qk_split = sem("mm_done"), sem("mm_taken"), sem("qk_split")
        qk_stored = [sem(f"qk_stored{n}") for n in range(4)]
        v_stored = [sem(f"v_stored{n}") for n in range(2)]
        dve = sem("dve")
        norm_step, stats_seen, hi_step, qk_hi_step = sem("norm_step"), sem("stats_seen"), sem("hi_step"), sem("qk_hi_step")

        x_blocks = x.rearrange("b (n t p) d -> (b n) p t d", t=TT, p=P)
        v_blocks = sh.v_rows.rearrange("(n t p) d -> n t p d", t=TT, p=P)
        wc_parts = Wc.rearrange("(t p) (c n) -> c p t n", p=P, n=H)
        PER_BLOCK = 2 * G + TT
        N_QK = 2 * G
        PARTS = (0, 1, 3, 4, 2, 5)
        RESULTS = (0, 1, 2, 3, 4, 6, 8)
        ROWS_AT = ((0, 2), (1, 3), (2, 4), (3, 5))
        RESULT_AT = ((1, 2, 0), (2, 3, 0), (3, 4, 0), (4, 4, 1), (5, 5, 0), (6, 5, 1))
        block = ctx.enter_context(nc.Block())

        @block.sync
        def _(sp):
            for r, v, n in ((ROW_BC, bc, 6 * KT), (ROW_BQ, bq, KT), (ROW_BK, bk, KT), (ROW_BV, bv, KT), (ROW_B1, b1, MT)):
                sp.dma_start(rows[r:r + n, :], v.rearrange("(r p) -> r p", p=P)).then_inc(rows_in, 16)
            sp.dma_start(rows[ROW_C:ROWS, :], c.rearrange("b (t p) -> (b t) p", p=P)).then_inc(rows_in, 16)
            sp.dma_start(xb[:, 0, :, :], x_blocks[0]).then_inc(x_in[0], 16)
            def load_wc(e):
                sp.dma_start(wc[:, e % 2, :, :], wc_parts[PARTS[e]]).then_inc(wc_in[e], 16)

            load_wc(0)
            load_wc(1)
            for n, w in enumerate((Wq, Wk, Wv)):
                sp.dma_start(w_raw[n], w.rearrange("(t p) n -> p t n", p=P)).then_inc(w_in[n], 16)
            sp.dma_start(xb[:, 1, :, :], x_blocks[1]).then_inc(x_in[1], 16)
            sp.wait_ge(c_done, 2)
            load_wc(2)
            load_wc(3)
            for n, v in enumerate((bc[2 * H:3 * H], bc[5 * H:6 * H], bo, b2)):
                sp.dma_start(bc_wide[:, n, :], v.rearrange("(a n) -> a n", a=1).broadcast_to([P, H])).then_inc(wide_in, 16)

            def store(k, i, q, load_next):
                for m in range(N_QK):
                    dst = (sh.q_parts, sh.k_parts)[m % 2]
                    group, tok = sp.snap(k // BPB * G + m // 2), sp.snap(k % BPB * TOK)
                    sp.wait_ge(qk_split, 2 + N_QK * k + m + 1)
                    sp.dma_start(dst[bass.ds(group, 1), :, :, bass.ds(tok, TOK)].rearrange("a p s n -> p (a s) n"),
                                 qk_out[:, m % 4, :, :].bitcast(F32)).then_inc(qk_stored[m % 4], 16)
                    if m == N_QK // 2 and load_next:
                        sp.wait_ge(t_done, KT * (k + 1) + 1)
                        sp.dma_start(xb[:, q, :, :], x_blocks[k + 2]).then_inc(x_in[q], 16)
                for t in range(TT):
                    sp.wait_ge(mm_taken, 4 + PER_BLOCK * k + N_QK + t + 1)
                    sp.dma_start(v_blocks[k, t], v_out[:, t % 2, :]).then_inc(v_stored[t % 2], 16)

            with sp.Fori(0, NBLK // 2 - 1) as i:
                for q in range(2):
                    store(2 * i + q, i, q, True)
            store(NBLK - 2, NBLK // 2 - 1, 0, False)
            for e in (4, 5):
                sp.wait_ge(c_done, e - 1)
                load_wc(e)
            for n in range(3):
                sp.wait_ge(w_split[n], 1)
            for s in qk_stored:
                sp.wait_ge(s, 1 + 16 * BPB * N_QK // 4)
            load_stacked(sp, sh.space[0].parts, sh.q_parts, Q_PARTS, 0, 0, next_in)
            for chunk in range(2):
                load_stacked(sp, sh.space[1 + chunk].parts, sh.k_parts, K_PARTS, 0, chunk * TOK, next_in)
            store(NBLK - 1, NBLK // 2 - 1, 1, False)
            sp.wait_ge(next_in, 16 * 9)
            for s in qk_stored:
                sp.wait_ge(s, 1 + 16 * NBLK * N_QK // 4)
            for s in v_stored:
                sp.wait_ge(s, 1 + 16 * NBLK * TT // 2)

        @block.gpsimd
        def _(pool):
            for s, n in ((t_taken, 2), (xm_split, 2), (mm_taken, 4), (qk_split, 2), (mm_done, 1)):
                pool.sem_inc(s, n)
            for s in qk_stored + v_stored:
                pool.sem_inc(s, 1)
            pool.memset(sh.ones[:, :], 1.0).then_inc(const_ready, 1)
            pool.memset(neg_half[:, :], -0.5).then_inc(const_ready, 1)
            pool.memset(sh.ident[:, :], 0.0).then_inc(const_ready, 1)
            pool.memset(c_silu[:, :, :], 0.0).then_inc(const_ready, 1)
            pool.wait_ge(const_ready, 4)
            pool.affine_select(out=sh.ident[:, :], in_=sh.ident[:, :], compare_op=ALU.not_equal, fill=1.0,
                               base=0, pattern=[[-1, P]], channel_multiplier=1).then_inc(const_ready, 1)

            def root(k):
                pool.wait_ge(stats_ready, k + 1)
                pool.tensor_tensor(rstd[:, :], var_eps[:, :], neg_half[:, :], ALU.pow).then_inc(rstd_ready, 1)

            root(0)
            pool.wait_ge(w_hi_ready, 1)
            pool.tensor_tensor(w_lo[:, 0, :, :], w_raw[0], w_hi[:, 0, :, :].bitcast(F32), ALU.subtract).then_inc(w_split[0], 1)
            with pool.Fori(1, NBLK) as k:
                root(k)

        @block.vector
        def _(v):
            steps = [0]

            def after(ins):
                steps[0] += 1
                ins.then_inc(dve, 1)
                v.wait_ge(dve, steps[0])

            def norm(k, i, q):
                v.wait_ge(x_in[q], 16 * i + 16)
                for t in range(TT):
                    last = v.bn_stats(stats[:, t, :], xb[:, q, t, :])
                last.then_inc(norm_step, 1)
                v.wait_ge(norm_step, 2 * k + 1)
                v.sem_inc(stats_seen, 1)
                for t in range(TT):
                    last = v.bn_aggr(mv[:, t, :], stats[:, t, :])
                last.then_inc(norm_step, 1)
                v.wait_ge(norm_step, 2 * k + 2)
                v.tensor_scalar(var_eps[:, :], mv[:, :, 1], EPS, None, ALU.add).then_inc(stats_ready, 1)
                v.wait_ge(rstd_ready, k + 1)
                for t in range(TT):
                    last = v.tensor_scalar(xb[:, q, t, :], xb[:, q, t, :], mv[:, t, 0:1], rstd[:, t:t + 1],
                                           ALU.subtract, ALU.mult)
                last.then_inc(xn_ready, 1)

            def split_xm(k, q):
                v.wait_ge(mm_done, PER_BLOCK * (k - 1) + 1) if not isinstance(k, int) or k > 1 else None
                for t in range(KT):
                    v.wait_ge(t_taken, 2 + KT * k + t + 1)
                    v.tensor_copy(xm_hi[:, q, t, :], xm[:, t % 2, :]).then_inc(hi_step, 1)
                    v.wait_ge(hi_step, KT * k + t + 1)
                    v.tensor_tensor(xm_lo[:, q, t, :], xm[:, t % 2, :], xm_hi[:, q, t, :].bitcast(F32),
                                    ALU.subtract).then_inc(xm_split, 1)

            def split_qk(k, ms):
                for m in ms:
                    v.wait_ge(mm_taken, 4 + PER_BLOCK * k + m + 1)
                    v.wait_ge(qk_stored[m % 4], 16 * (k * N_QK // 4 + m // 4) + 1)
                    v.tensor_copy(qk_out[:, m % 4, 0, :], qk[:, m % 2, :]).then_inc(qk_hi_step, 1)
                    v.wait_ge(qk_hi_step, N_QK * k + m + 1)
                    v.tensor_tensor(qk_out[:, m % 4, 1, :], qk[:, m % 2, :], qk_out[:, m % 4, 0, :].bitcast(F32),
                                    ALU.subtract).then_inc(qk_split, 1)

            v.wait_ge(rows_t, 1)
            after(v.tensor_copy(sh.vecs[:, :], c_bank[:, 0:ROWS]))
            v.tensor_scalar(sh.bq_scaled[:, :], sh.vecs[:, ROW_BQ:ROW_BQ + KT], 1.0 / DH, None, ALU.mult).then_inc(vecs_ready, 1)
            v.wait_ge(const_ready, 5)
            after(v.tensor_reduce(select[:, :], sh.ident[:, :].rearrange("p (s r) -> p r s", s=KT)[:, 0:B, :], AX.X, ALU.add))
            for b in range(B):
                last = v.tensor_scalar(select_wide[:, b, :], sh.ones[:, :], select[:, b:b + 1], None, ALU.mult)
            last.then_inc(select_ready, 1)
            norm(0, 0, 0)

            def mod_columns(e, column, one):
                v.wait_ge(g_done, RESULTS[e] + 1)
                part = PARTS[e]
                for b in range(B):
                    last = v.tensor_tensor(sh.mod[:, b, column:column + KT], g_bank[:, :].rearrange("p (t b) -> p b t", t=H // 2)[:, b, 0:KT],
                                           sh.vecs[:, ROW_BC + part * KT:ROW_BC + (part + 1) * KT], ALU.add)
                if one:
                    after(last)
                    last = v.tensor_scalar(sh.mod[:, :, column:column + KT], sh.mod[:, :, column:column + KT], 1.0, None, ALU.add)
                last.then_inc(g_taken, 1)

            def gate(e, b):
                wide, gate, bias = ((0, G_MSA, GBO), (1, G_MLP, GB2))[e - 4]
                v.wait_ge(wide_in, 16 * 4)
                v.wait_ge(g_done, RESULTS[e] + b + 1)
                after(v.tensor_tensor(sh.gates[:, b, gate, :], g_bank[:, :], bc_wide[:, wide, :], ALU.add))
                v.tensor_tensor(sh.gates[:, b, bias, :], sh.gates[:, b, gate, :], bc_wide[:, 2 + wide, :], ALU.mult).then_inc(g_taken, 1)

            def result(e, b):
                if e == 2:
                    mod_columns(e, SHIFT_MLP, False)
                elif e == 3:
                    mod_columns(e, SCALE_MLP, True)
                else:
                    gate(e, b)

            def high_w(n):
                v.wait_ge(w_in[n], 16)
                return v.tensor_copy(w_hi[:, n, :, :], w_raw[n])

            mod_columns(0, SHIFT_MSA, False)
            high_w(0).then_inc(w_hi_ready, 1)
            mod_columns(1, SCALE_MSA, True)
            split_xm(0, 0)
            for n in (1, 2):
                after(high_w(n))
                v.tensor_tensor(w_lo[:, n, :, :], w_raw[n], w_hi[:, n, :, :].bitcast(F32), ALU.subtract).then_inc(w_split[n], 1)

            def body(k, i, q, has_next):
                if has_next:
                    norm(k + 1, i + q, 1 - q)
                split_qk(k, range(N_QK // 2))
                if has_next:
                    split_xm(k + 1, 1 - q)
                split_qk(k, range(N_QK // 2, N_QK))

            with v.Fori(0, NBLK // 2 - 1) as i:
                for q in range(2):
                    body(2 * i + q, i, q, True)
            body(NBLK - 2, NBLK // 2 - 1, 0, True)
            for m in range(N_QK):
                split_qk(NBLK - 1, (m,))
                for at, e, b in RESULT_AT:
                    if at == m:
                        result(e, b)

        @block.scalar
        def _(act):
            act.wait_ge(vecs_ready, 1)
            act.wait_ge(const_ready, 5)
            act.activation(c_silu[:, :, 0:B], sh.vecs[:, ROW_C:ROWS].rearrange("p (b s) -> p s b", s=KT), ACT.Silu).then_inc(silu_ready, 1)

            def take_rows(e):
                act.wait_ge(c_done, e + 1)
                if e >= 2:
                    act.wait_ge(g_done, RESULTS[e - 1])
                act.activation(c_part[:, e % 2, :], c_bank[:, :], ACT.Copy).then_inc(c_taken, 1)

            def modulate(k, b, t0=0):
                for t in range(KT):
                    act.wait_ge(t_done, KT * k + t + 1)
                    act.wait_ge(xm_split, KT * k + t + 1)
                    act.activation(xm[:, t % 2, :], t_bank[t % 2][:, :], ACT.Identity,
                                   scale=sh.mod[:, bass.ds(b, 1), SCALE_MSA + t].rearrange("p a -> p (a)"),
                                   bias=sh.mod[:, bass.ds(b, 1), SHIFT_MSA + t].rearrange("p a -> p (a)")).then_inc(t_taken, 1)

            def take_qk(k, ms):
                for m in ms:
                    act.wait_ge(mm_done, 1 + PER_BLOCK * k + m + 1)
                    act.wait_ge(qk_split, N_QK * k + m + 1)
                    g = m // 2
                    if m % 2 == 0:
                        ins = act.activation(qk[:, 0, :], mm_bank[m % 4][:, :], ACT.Identity,
                                             scale=1.0 / DH, bias=sh.bq_scaled[:, g:g + 1])
                    else:
                        ins = act.activation(qk[:, 1, :], mm_bank[m % 4][:, :], ACT.Identity,
                                             bias=sh.vecs[:, ROW_BK + g:ROW_BK + g + 1])
                    ins.then_inc(mm_taken, 1)

            def body(k, next_b, has_next):
                if not has_next:
                    for m in range(N_QK // 2):
                        take_qk(k, (m,))
                        for at, e in ROWS_AT:
                            if at == m:
                                take_rows(e)
                else:
                    take_qk(k, range(N_QK // 2))
                if has_next:
                    modulate(k + 1, next_b)
                take_qk(k, range(N_QK // 2, N_QK))
                for t in range(TT):
                    act.wait_ge(mm_done, 1 + PER_BLOCK * k + N_QK + t + 1)
                    act.wait_ge(v_stored[t % 2], 16 * (k * TT // 2 + t // 2) + 1)
                    act.activation(v_out[:, t % 2, :], mm_bank[(N_QK + t) % 4][:, :], ACT.Copy).then_inc(mm_taken, 1)

            take_rows(0)
            take_rows(1)
            act.wait_ge(g_taken, 2)
            modulate(0, 0)
            with act.Fori(0, NBLK // 2 - 1) as i:
                for q in range(2):
                    body(2 * i + q, (2 * i + q + 1) // BPB, True)
            body(NBLK - 2, B - 1, True)
            body(NBLK - 1, 0, False)

        @block.tensor
        def _(pe):
            pe.wait_ge(rows_in, 16 * 6)
            pe.wait_ge(const_ready, 5)
            pe.transpose(c_bank[:, 0:ROWS], rows[:, :], sh.ident[0:ROWS, 0:ROWS]).then_inc(rows_t, 1)

            def part_rows(e):
                pe.wait_ge(wc_in[e], 16)
                if e:
                    pe.wait_ge(c_taken, e)
                for s in range(KT):
                    last = pe.matmul(c_bank[s * P // KT:(s + 1) * P // KT, :], c_silu[:, s, :], wc[:, e % 2, s, :], start=True, stop=True)
                last.then_inc(c_done, 1)

            def part_columns(e):
                pe.wait_ge(c_taken, e + 1)
                if e:
                    pe.wait_ge(g_taken, RESULTS[e])
                for t in range(KT):
                    last = pe.matmul(g_bank[:, t * B:(t + 1) * B], c_part[:, e % 2, t * P:(t + 1) * P], select[:, :], start=True, stop=True)
                last.then_inc(g_done, 1)

            def part_wide(e, b):
                pe.wait_ge(c_taken, e + 1)
                pe.wait_ge(g_taken, RESULTS[e] + b)
                pe.matmul(g_bank[:, :], select_wide[:, b, :], c_part[:, e % 2, :], start=True, stop=True).then_inc(g_done, 1)

            def transposes(k, q):
                pe.wait_ge(xn_ready, k + 1)
                for t in range(KT):
                    pe.wait_ge(t_taken, KT * k + t + 1)
                    for s in range(TT):
                        last = pe.transpose(t_bank[t % 2][:, s * P:(s + 1) * P], xb[:, q, s, t * P:(t + 1) * P], sh.ident[:, :])
                    last.then_inc(t_done, 1)

            def three(bank, hi_l, lo_l, hi_r, lo_r):
                for t in range(KT):
                    pe.matmul(bank, hi_l(t), hi_r(t), start=(t == 0), stop=False)
                    pe.matmul(bank, hi_l(t), lo_r(t), start=False, stop=False)
                    last = pe.matmul(bank, lo_l(t), hi_r(t), start=False, stop=(t == KT - 1))
                last.then_inc(mm_done, 1)

            def products(k, q, ms):
                for m in ms:
                    pe.wait_ge(mm_taken, PER_BLOCK * k + m + 1)
                    pe.wait_ge(w_split[m % 2 if m < N_QK else 2], 1)
                    bank = mm_bank[m % 4][:, :]
                    if m < N_QK:
                        n, g = m % 2, m // 2
                        three(bank, lambda t: w_hi[:, n, t, g * P:(g + 1) * P], lambda t: w_lo[:, n, t, g * P:(g + 1) * P],
                              lambda t: xm_hi[:, q, t, :], lambda t: xm_lo[:, q, t, :])
                    else:
                        s = m - N_QK
                        three(bank, lambda t: xm_hi[:, q, t, s * P:(s + 1) * P], lambda t: xm_lo[:, q, t, s * P:(s + 1) * P],
                              lambda t: w_hi[:, 2, t, :], lambda t: w_lo[:, 2, t, :])

            def body(k, q, has_next):
                pe.wait_ge(xm_split, 2 + KT * (k + 1))
                products(k, q, range(N_QK // 2))
                if has_next:
                    transposes(k + 1, 1 - q)
                products(k, q, range(N_QK // 2, PER_BLOCK))

            pe.wait_ge(silu_ready, 1)
            part_rows(0)
            pe.wait_ge(select_ready, 1)
            part_columns(0)
            part_rows(1)
            part_columns(1)
            transposes(0, 0)
            with pe.Fori(0, NBLK // 2 - 1) as i:
                for q in range(2):
                    body(2 * i + q, q, True)
            body(NBLK - 2, 0, True)
            pe.wait_ge(xm_split, 2 + KT * NBLK)
            for m in range(PER_BLOCK):
                products(NBLK - 1, 1, (m,))
                for at, e in ROWS_AT:
                    if at == m:
                        part_rows(e)
                for at, e, b in RESULT_AT:
                    if at == m:
                        part_columns(e) if e < 4 else part_wide(e, b)


STACK = 3 * DH
Q_PARTS, K_PARTS = (0, 0, 1), (0, 1, 0)
N_IT = B * G * BPB
N_MAX = BPB * HPG * TT
CHUNK = TOK // P
N_PAIR = NKT // 2


def attend(nc, sh, late, x, Wo, W1):
    with ExitStack() as ctx:
        def sb(name, shape, dt=F32):
            return ctx.enter_context(nc.sbuf_tensor(name, shape, dt))

        def pb(name, shape):
            return ctx.enter_context(nc.psum_tensor(name, shape, F32))

        def sem(name):
            return ctx.enter_context(nc.semaphore(name))

        km_space, qm_space = [*sh.space[1:3], *late.space[0:2]], [sh.space[0], late.space[2]]
        km = [t.parts for t in km_space]
        ks = sb("ks", [STACK + 1, HPG, S], F32R)
        qm = [t.parts for t in qm_space]
        qs = [sb(f"qs{u}", [STACK + 1, HPG, TOK], F32R) for u in range(2)]
        vs = sb("vs", [P, NKT, P])
        probs = sb("probs", [P, 4, HPG, TOK])
        pair_sum = sb("pair_sum", [P, 2, 2, HPG, TOK])
        part_max = sb("part_max", [P, 2, HPG * TT, BPB])
        neg_max = sb("neg_max", [P, HPG * TT])
        neg_max_row = sb("neg_max_row", [HPG * TT, P], F32R)
        y_raw = sb("y_raw", [P, 2, TOK])
        d_raw, inv = sb("d_raw", [P, TOK]), sb("inv", [P, TOK])
        d_small, inv_small = sb("d_small", [P, HPG * TOK // P]), sb("inv_small", [P, HPG * TOK // P])
        y_out = sb("y_out", [P, 2, TOK])

        s_bank = [pb(f"s_bank{n}", [P, TOK]) for n in range(3)]
        y_bank = pb("y_bank", [P, TOK])
        d_bank = pb("d_bank", [P, TOK])
        m_bank = [pb(f"m_bank{n}", [P, TOK]) for n in range(3)]

        km_in = [sem(f"km_in{c}") for c in range(BPB)]
        ks_in = [sem(f"ks_in{c}") for c in range(BPB)]
        v_in = [sem(f"v_in{c}") for c in range(BPB)]
        qm_in = [sem(f"qm_in{u}") for u in range(2)]
        qs_in = [sem(f"qs_in{u}") for u in range(2)]
        row_in = [sem(f"row_in{u}") for u in range(2)]
        ones_row = sem("ones_row")
        s_done, p_done, av_done, pair_ready, d_done = sem("s_done"), sem("p_done"), sem("av_done"), sem("pair_ready"), sem("d_done")
        quad_low, quad_high, pair_low = sem("quad_low"), sem("quad_high"), sem("pair_low")
        y_taken, d_taken, y_normed, inv_ready = sem("y_taken"), sem("d_taken"), sem("y_normed"), sem("inv_ready")
        d_moved, small_ready, inv_stored, inv_in = sem("d_moved"), sem("small_ready"), sem("inv_stored"), sem("inv_in")
        y_stored = [sem(f"y_stored{u}") for u in range(2)]
        m_done, m_taken, neg_ready = sem("m_done"), sem("m_taken"), sem("neg_ready")
        wo_in, next_in = sem("wo_in"), sem("next_in")
        LEAD = 12
        N_QUAD, N_SC = N_PAIR // 2, HPG * NKT
        M_USES = N_MAX + 1
        BEFORE = 3

        def place(i, n):
            return n + (1 if n >= BEFORE or (isinstance(i, int) and i == 0) else 0)

        def place_transposed(i):
            return 0 if isinstance(i, int) and i == N_IT - 1 else BEFORE

        def max_done(i, n):
            return M_USES * i + place(i, n)

        def transposed_done(i):
            return M_USES * (i + 1) + place_transposed(i)

        TAKEN = 3

        def before(at):
            return 2 if at < 2 else 3

        block = ctx.enter_context(nc.Block())

        @block.sync
        def _(sp):
            def load_km(group, c):
                load_stacked(sp, km[c], sh.k_parts, K_PARTS, group, c * TOK, km_in[c])

            def load_ks(group, c):
                load_stacked(sp, ks[:, :, c * TOK:(c + 1) * TOK], sh.k_parts, K_PARTS, group, c * TOK, ks_in[c])

            def load_v(group, c):
                row, col = sp.snap(group // G * S + c * TOK), sp.snap(group % G * P)
                sp.dma_start(vs[:, c * CHUNK:(c + 1) * CHUNK, :],
                             sh.v_rows[bass.ds(row, TOK), bass.ds(col, P)].rearrange("(t p) n -> p t n", p=P)).then_inc(v_in[c], 16)

            def load_qm(group, qt):
                u = qt % 2
                load_stacked(sp, qm[u], sh.q_parts, Q_PARTS, group, qt * TOK, qm_in[u])

            def load_qs(group, qt):
                u = qt % 2
                load_stacked(sp, qs[u], sh.q_parts, Q_PARTS, group, qt * TOK, qs_in[u])

            def load_row(u):
                sp.dma_start(qs[u][STACK:STACK + 1, :, :].rearrange("a h n -> a (h n)").bitcast(F32),
                             neg_max_row[:, :].bitcast(F32)).then_inc(row_in[u], 16)

            def iteration(group, qt, last_group):
                i = BPB * group + qt
                following = [(group + (qt + d) // BPB, (qt + d) % BPB) for d in (1, 2)]
                there = [not (last_group and qt + d >= BPB) for d in (1, 2)]
                if there[1]:
                    sp.wait_ge(m_done, max_done(i, N_MAX - 1))
                    load_qm(*following[1])
                if there[0]:
                    sp.wait_ge(s_done, 1 + N_SC * i)
                    load_qs(*following[0])
                for c in range(BPB - 1 if qt == BPB - 1 else BPB):
                    if qt == BPB - 2 and not last_group:
                        sp.wait_ge(m_done, max_done(i + 1, HPG * TT * (c + 1) - 1))
                        load_km(group + 1, c)
                    if qt == BPB - 1 and not last_group:
                        sp.wait_ge(s_done, 1 + N_SC * i + HPG * CHUNK * (c + 1))
                        load_ks(group + 1, c)
                        sp.wait_ge(av_done, 4 + NKT * i + CHUNK * (c + 1))
                        load_v(group + 1, c)
                if there[0]:
                    sp.wait_ge(m_taken, TAKEN + transposed_done(i + 1))
                    load_row((qt + 1) % 2)
                if qt == BPB - 1 and not last_group:
                    c = BPB - 1
                    sp.wait_ge(s_done, 1 + N_SC * (i + 1))
                    load_ks(group + 1, c)
                    sp.wait_ge(av_done, 4 + NKT * (i + 1))
                    load_v(group + 1, c)

            for c in (2, 3):
                load_km(0, c)
            load_qm(0, 1)
            load_qs(0, 0)
            for c in range(BPB):
                load_ks(0, c)
                load_v(0, c)
            sp.dma_start(late.wo[:, :, :], Wo.rearrange("(t p) n -> p t n", p=P)).then_inc(wo_in, 16)
            sp.wait_ge(m_taken, TAKEN + transposed_done(0))
            load_row(0)
            with sp.Fori(0, B * G - 1) as group:
                for qt in range(BPB):
                    iteration(group, qt, False)
            for qt in range(BPB - 1):
                iteration(B * G - 1, qt, True)
            sp.wait_ge(m_done, max_done(N_IT - 1, N_MAX - 1))
            for c in range(BPB):
                cols = slice(c * MLP // 4, (c + 1) * MLP // 4)
                sp.dma_start(km_space[c].plain[:, :, :], W1[:, cols].rearrange("(t p) n -> p t n", p=P)).then_inc(next_in, 16)
            sp.wait_ge(y_stored[0], 1 + 16 * ((G - 1) * BPB // 2 + 1))
            sp.dma_start(qm_space[0].plain[:, :, :], sh.y_cols[0:G, :, 0:TOK].rearrange("g p n -> p g n")).then_inc(next_in, 16)
            sp.dma_start(qm_space[1].plain[:, :, :], x[0, 0:TOK, :].rearrange("(t p) d -> p t d", p=P)).then_inc(next_in, 16)
            iteration(B * G - 1, BPB - 1, True)
            sp.wait_ge(next_in, 16 * (BPB + 2))
            sp.wait_ge(wo_in, 16)
            for u in range(2):
                sp.wait_ge(y_stored[u], 1 + 16 * N_IT // 2)

        @block.gpsimd
        def _(pool):
            for s, n in ((s_done, 1), (p_done, 2), (av_done, 4), (pair_ready, 2), (d_done, 2), (y_taken, 1),
                         (d_taken, 1), (y_normed, 2), (m_taken, TAKEN), (d_moved, 1), (inv_stored, 1), (inv_in, 1),
                         (y_stored[0], 1), (y_stored[1], 1)):
                pool.sem_inc(s, n)
            for s in (km_in[0], km_in[1], qm_in[0]):
                pool.sem_inc(s, 16 * 3)
            pool.memset(ks[STACK:STACK + 1, :, :].bitcast(F32), 1.0).then_inc(ones_row, 1)
            def body(i, last):
                for j in range(N_PAIR):
                    q, half = j // 2, j % 2
                    if half == 0:
                        pool.wait_ge(d_done, N_QUAD * i + q + 1)
                    for r in (1,) if last else (0, 1):
                        pool.wait_ge(p_done, 2 + N_SC * i + HPG * (2 * j + 1) + 2 * r + 2)
                        ins = pool.tensor_tensor(pair_sum[:, q % 2, half, 2 * r:2 * r + 2, :], probs[:, 2 * j % 4, 2 * r:2 * r + 2, :],
                                                 probs[:, (2 * j + 1) % 4, 2 * r:2 * r + 2, :], ALU.add)
                    ins.then_inc(pair_ready, 1)
                    if half == 1:
                        pool.wait_ge(pair_ready, 2 + N_PAIR * i + j + 1)
                        pool.tensor_tensor(pair_sum[:, q % 2, 0, 2:4, :], pair_sum[:, q % 2, 0, 2:4, :],
                                           pair_sum[:, q % 2, 1, 2:4, :], ALU.add).then_inc(quad_high, 1)

            with pool.Fori(0, N_IT - 1) as i:
                body(i, False)
            body(N_IT - 1, True)

        @block.scalar
        def _(act):
            def take_y(i, u):
                act.wait_ge(av_done, 4 + NKT * (i + 1))
                act.wait_ge(y_normed, i + 1)
                act.activation(y_raw[:, u, :], y_bank[:, :], ACT.Copy).then_inc(y_taken, 1)

            def take_sums(i):
                act.wait_ge(d_done, 2 + N_QUAD * (i + 1))
                act.wait_ge(d_moved, 16 * i + 1)
                act.activation(d_raw[:, :], d_bank[:, :], ACT.Copy).then_inc(d_taken, 1)

            def move_sums(i):
                act.wait_ge(d_taken, 1 + i + 1)
                act.dma_start(d_small[:, :], d_raw[0:P:DH, :]).then_inc(d_moved, 16)

            def store_inv(i):
                act.wait_ge(small_ready, i + 1)
                act.wait_ge(inv_in, 16 * i + 1)
                act.dma_start(sh.inv_rows, inv_small[:, :]).then_inc(inv_stored, 16)

            def load_inv(i):
                act.wait_ge(inv_stored, 16 * (i + 1) + 1)
                act.wait_ge(y_normed, 2 + i)
                act.dma_start(inv[:, :], sh.inv_rows.rearrange("h (a n) -> h a n", a=1).broadcast_to([HPG, DH, TOK])).then_inc(inv_in, 16)

            def store_y(i, u):
                group, tok = act.snap(i // BPB), act.snap(i % BPB * TOK)
                act.wait_ge(y_normed, 2 + i + 1)
                act.dma_start(sh.y_cols[bass.ds(group, 1), :, bass.ds(tok, TOK)].rearrange("a p n -> p (a n)"),
                              y_out[:, u, :]).then_inc(y_stored[u], 16)

            def body(i, u, has_prev, last=False):
                for t in range(NKT):
                    for h in range(HPG):
                        act.wait_ge(s_done, 1 + N_SC * i + HPG * t + h + 1)
                        if h == 0:
                            act.wait_ge(av_done, NKT * i + t + 1)
                            act.wait_ge(pair_ready, N_PAIR * i + t // 2 + 1)
                            if last and t >= 4:
                                act.wait_ge(pair_low, t // 2 - 1)
                        act.activation(probs[:, t % 4, h, :], s_bank[(HPG * t + h) % 3][:, :], ACT.Exp).then_inc(p_done, 1)
                    if t == 0 and has_prev:
                        take_y(i - 1, 1 - u)
                    if t == 4 and has_prev:
                        take_sums(i - 1)
                    if t == 5 and has_prev:
                        move_sums(i - 1)
                    if t == 8 and has_prev:
                        store_inv(i - 1)
                    if t == 10 and has_prev:
                        load_inv(i - 1)
                    if t == 14 and has_prev:
                        store_y(i - 1, 1 - u)

            body(0, 0, False)
            with act.Fori(0, N_IT // 2 - 2) as j:
                body(2 * j + 1, 1, True)
                body(2 * j + 2, 0, True)
            for i in range(N_IT - 3, N_IT):
                body(i, i % 2, True, i == N_IT - 1)
            take_y(N_IT - 1, 1)
            take_sums(N_IT - 1)
            store_y(N_IT - 1, 1)

        @block.vector
        def _(v):
            def maximum(i, u, n):
                c, hs = n // (HPG * TT), n % (HPG * TT)
                v.wait_ge(m_done, max_done(i, n))
                v.tensor_reduce(part_max[:, u, hs, c:c + 1], m_bank[place(i, n) % 3][:, :], AX.X, ALU.max).then_inc(m_taken, 1)

            def negative(i, u):
                v.wait_ge(m_taken, TAKEN + max_done(i, N_MAX - 1))
                v.tensor_reduce(neg_max[:, :], part_max[:, u, :, :], AX.X, ALU.max, negate=True).then_inc(neg_ready, 1)

            def as_row(i, row_before=None):
                v.wait_ge(m_done, transposed_done(i))
                if row_before is not None:
                    v.wait_ge(*row_before)
                v.tensor_copy(neg_max_row[:, :], m_bank[place_transposed(i) % 3][0:HPG * TT, 0:P]).then_inc(m_taken, 1)

            def quad(i, q):
                v.wait_ge(pair_ready, 2 + N_PAIR * i + 2 * q + 2)
                v.tensor_tensor(pair_sum[:, q % 2, 0, 0:2, :], pair_sum[:, q % 2, 0, 0:2, :],
                                pair_sum[:, q % 2, 1, 0:2, :], ALU.add).then_inc(quad_low, 1)

            QUAD_AT, INVERT_AT, NORMALISE_AT = (44, 60, 10, 28), 40, 59
            QUARTER = TOK // 4

            def invert_small(i):
                v.wait_ge(d_moved, 16 * (i + 1) + 1)
                v.wait_ge(inv_stored, 16 * i + 1)
                v.reciprocal(inv_small[:, :], d_small[:, :]).then_inc(small_ready, 1)

            def invert_last(n):
                if n == 0:
                    v.wait_ge(d_taken, 1 + N_IT)
                s = slice(n * QUARTER, (n + 1) * QUARTER)
                v.reciprocal(inv[:, s], d_raw[:, s]).then_inc(inv_ready, 1)

            def normalise(i, u, inv_there):
                v.wait_ge(y_taken, 1 + i + 1)
                v.wait_ge(y_stored[u], 16 * (i // 2) + 1)
                v.wait_ge(*inv_there)
                v.tensor_tensor(y_out[:, u, :], y_raw[:, u, :], inv[:, :], ALU.mult).then_inc(y_normed, 1)

            def body(i, u, has_prev, ahead):
                after = {(1, QUAD_AT[0]): [lambda: quad(i, 0)], (1, QUAD_AT[1]): [lambda: quad(i, 1)], (2, QUAD_AT[2]): [lambda: quad(i, 2)]}
                if has_prev:
                    after[1, QUAD_AT[3]] = [lambda: quad(i - 1, 3)]
                    after[1, INVERT_AT] = [lambda: invert_small(i - 1)]
                    after[1, NORMALISE_AT] = [lambda: normalise(i - 1, 1 - u, (inv_in, 16 * i + 1))]

                def step(d, n):
                    if d <= ahead:
                        maximum(i + d, (u + d) % 2, n)
                    for work in after.get((d, n), ()):
                        work()

                for n in range(LEAD, N_MAX):
                    step(1, n)
                if ahead >= 1:
                    negative(i + 1, 1 - u)
                if ahead >= 2:
                    for n in range(BEFORE):
                        step(2, n)
                if ahead >= 1:
                    as_row(i + 1, (row_in[u], 16 * (i // 2 + 1)))
                for n in range(BEFORE if ahead >= 2 else 0, LEAD):
                    step(2, n)

            for n in range(N_MAX):
                maximum(0, 0, n)
            negative(0, 0)
            for n in range(BEFORE):
                maximum(1, 1, n)
            as_row(0)
            for n in range(BEFORE, LEAD):
                maximum(1, 1, n)
            body(0, 0, False, 2)
            with v.Fori(0, N_IT // 2 - 2) as j:
                body(2 * j + 1, 1, True, 2)
                body(2 * j + 2, 0, True, 2)
            for i in range(N_IT - 3, N_IT - 1):
                body(i, i % 2, True, N_IT - 1 - i)

            def last_pair(j):
                q, half = j // 2, j % 2
                v.wait_ge(p_done, 2 + N_SC * (N_IT - 1) + HPG * (2 * j + 1) + 2)
                v.wait_ge(d_done, N_QUAD * (N_IT - 1) + q + 1)
                v.tensor_tensor(pair_sum[:, q % 2, half, 0:2, :], probs[:, 2 * j % 4, 0:2, :], probs[:, (2 * j + 1) % 4, 0:2, :],
                                ALU.add).then_inc(pair_low, 1)

            def last_quad(q):
                for j in (2 * q, 2 * q + 1):
                    last_pair(j)
                v.wait_ge(pair_low, 2 * q + 2)
                quad(N_IT - 1, q)

            quad(N_IT - 2, 3)
            last_quad(0)
            invert_small(N_IT - 2)
            last_quad(1)
            last_quad(2)
            normalise(N_IT - 2, 0, (inv_in, 16 * (N_IT - 1) + 1))
            last_quad(3)
            for n in range(4):
                invert_last(n)
            normalise(N_IT - 1, 1, (inv_ready, 4))

        @block.tensor
        def _(pe):
            def max_product(i, u, n):
                c, h, s = n // (HPG * TT), n // TT % HPG, n % TT
                if n == 0:
                    pe.wait_ge(qm_in[u], 16 * 3 * (i // 2 + 1))
                if n % (HPG * TT) == 0:
                    pe.wait_ge(km_in[c], 16 * 3 * (i // BPB + 1))
                pe.wait_ge(m_taken, TAKEN + max_done(i, n) - before(place(i, n)))
                pe.matmul(m_bank[place(i, n) % 3][:, :], qm[u][0:STACK, h, s * P:(s + 1) * P], km[c][0:STACK, h, :],
                          start=True, stop=True).then_inc(m_done, 1)

            def max_transpose(i):
                pe.wait_ge(neg_ready, i + 1)
                pe.wait_ge(m_taken, TAKEN + transposed_done(i) - before(place_transposed(i)))
                pe.transpose(m_bank[place_transposed(i) % 3][0:HPG * TT, 0:P], neg_max[:, :], sh.ident[:, :]).then_inc(m_done, 1)

            def scores(i, u, t, h):
                if h == 0 and t % CHUNK == 0:
                    pe.wait_ge(ks_in[t // CHUNK], 16 * 3 * (i // BPB + 1))
                n = HPG * t + h
                pe.wait_ge(p_done, 2 + N_SC * i + n + 1 - (1 if n == 0 else 3))
                pe.matmul(s_bank[n % 3][:, :], ks[:, h, t * P:(t + 1) * P], qs[u][:, h, :], start=True, stop=True).then_inc(s_done, 1)

            def times_v(i, t):
                if t % CHUNK == 0:
                    pe.wait_ge(v_in[t // CHUNK], 16 * (i // BPB + 1))
                if t == 0:
                    pe.wait_ge(y_taken, i + 1)
                pe.wait_ge(p_done, 2 + N_SC * i + HPG * (t + 1))
                for h in range(HPG):
                    last = pe.matmul(y_bank[h * DH:(h + 1) * DH, :], vs[:, t, h * DH:(h + 1) * DH], probs[:, t % 4, h, :],
                                     start=(t == 0), stop=(t == NKT - 1))
                last.then_inc(av_done, 1)

            def sums(i, q):
                if q == 0:
                    pe.wait_ge(d_taken, i + 1)
                pe.wait_ge(quad_low, N_QUAD * i + q + 1)
                pe.wait_ge(quad_high, N_QUAD * i + q + 1)
                for h in range(HPG):
                    last = pe.matmul(d_bank[h * DH:(h + 1) * DH, :], sh.ones[:, 0:DH], pair_sum[:, q % 2, 0, h, :],
                                     start=(q == 0), stop=(q == N_QUAD - 1))
                last.then_inc(d_done, 1)

            LATE = 2

            def body(i, u, has_prev, ahead):
                pe.wait_ge(qs_in[u], 16 * 3 * (i // 2 + 1))
                pe.wait_ge(row_in[u], 16 * (i // 2 + 1))
                left = []
                if ahead >= 1:
                    left = [lambda n=n: max_product(i + 1, 1 - u, n) for n in range(LEAD, N_MAX)]
                if ahead >= 2:
                    left += [lambda n=n: max_product(i + 2, u, n) for n in range(BEFORE)]
                if ahead >= 1:
                    left += [lambda: None] * (BEFORE if ahead == 1 else 0) + [lambda: max_transpose(i + 1)]
                if ahead >= 2:
                    left += [lambda n=n: max_product(i + 2, u, n) for n in range(BEFORE, LEAD)]

                def some_more(n):
                    for step in left[:n]:
                        step()
                    del left[:n]

                for t in range(NKT):
                    for h in range(HPG):
                        scores(i, u, t, h)
                        some_more(1)
                    if t > 0:
                        times_v(i, t - 1)
                    elif has_prev:
                        times_v(i - 1, NKT - 1)
                    if t % 4 == 0:
                        q = t // 4 - LATE
                        if q >= 0:
                            sums(i, q)
                        elif has_prev:
                            sums(i - 1, N_QUAD + q)
                some_more(len(left))

            for n in range(N_MAX):
                max_product(0, 0, n)
            for n in range(BEFORE):
                max_product(1, 1, n)
            max_transpose(0)
            for n in range(BEFORE, LEAD):
                max_product(1, 1, n)
            pe.wait_ge(ones_row, 1)
            body(0, 0, False, 2)
            with pe.Fori(0, N_IT // 2 - 2) as j:
                body(2 * j + 1, 1, True, 2)
                body(2 * j + 2, 0, True, 2)
            for i in range(N_IT - 3, N_IT):
                body(i, i % 2, True, min(2, N_IT - 1 - i))
            times_v(N_IT - 1, NKT - 1)
            for q in range(N_QUAD - LATE, N_QUAD):
                sums(N_IT - 1, q)


def feed_forward(nc, sh, late, x, W2, out):
    with ExitStack() as ctx:
        def sb(name, shape, dt=F32):
            return ctx.enter_context(nc.sbuf_tensor(name, shape, dt))

        def pb(name, shape):
            return ctx.enter_context(nc.psum_tensor(name, shape, F32))

        def sem(name):
            return ctx.enter_context(nc.semaphore(name))

        w1_raw = [t.plain for t in (*sh.space[1:3], *late.space[0:2])]
        w2_raw = sb("w2_raw", [P, MT, H])
        w1_hi, w1_lo = sb("w1_hi", [P, 2, KT, P], F32R), sb("w1_lo", [P, 2, KT, P], F32R)
        w2_hi, w2_lo = sb("w2_hi", [P, 2, H], F32R), sb("w2_lo", [P, 2, H], F32R)
        wo_hi, wo_lo = sb("wo_hi", [P, KT, H], F32R), sb("wo_lo", [P, KT, H], F32R)
        yb = sh.space[0].plain
        y_hi, y_lo = sb("y_hi", [P, KT, TOK], F32R), sb("y_lo", [P, KT, TOK], F32R)
        xb = [late.space[2].plain, sb("xb2", [P, TT, H])]
        stats, mv = sb("stats2", [P, TT, 6]), sb("mv2", [P, TT, 2])
        var_eps, rstd, neg_half = sb("var_eps2", [P, TT]), sb("rstd2", [P, TT]), sb("neg_half2", [P, TT])
        xn = late.wo
        xm = sb("xm2", [P, KT, TOK])
        xm_hi, xm_lo = sb("xm2_hi", [P, KT, TOK], F32R), sb("xm2_lo", [P, KT, TOK], F32R)
        h = sb("h", [P, 2, TOK])
        h_hi, h_lo = sb("h_hi", [P, 2, TOK], F32R), sb("h_lo", [P, 2, TOK], F32R)
        gated = sb("gated", [P, TT, H])

        acc_bank = [pb(f"acc_bank{t}", [P, H]) for t in range(TT)]
        up_bank = [pb(f"up_bank{n}", [P, TOK]) for n in range(2)]
        o_bank = pb("o_bank", [P, H])
        t_bank = pb("t_bank", [P, TOK])

        w2_in = [sem(f"w2_in{c}") for c in range(4)]
        y_in = [sem(f"y_in{g}") for g in range(G)]
        first_o, first_t = acc_bank, [up_bank[0], t_bank, o_bank, up_bank[1]]
        x_in = [sem(f"x2_in{q}") for q in range(2)]
        stored = [sem(f"stored{q}") for q in range(2)]
        wo_hi_ready, wo_split, half_ready = sem("wo_hi_ready"), sem("wo_split"), sem("half_ready")
        y_biased, y_split, y_hi_step = sem("y_biased"), sem("y_split"), sem("y_hi_step")
        x_biased, wo_done, wo_taken, gated_step, x1_step = sem("x_biased"), sem("wo_done"), sem("wo_taken"), sem("gated_step"), sem("x1_step")
        norm_step, stats_seen, stats_ready, rstd_ready, xn_ready, x1_biased = (
            sem("norm_step2"), sem("stats_seen2"), sem("stats_ready2"), sem("rstd_ready2"), sem("xn_ready2"), sem("x1_biased"))
        t_done, t_taken, xm_hi_step, xm_split = sem("t_done2"), sem("t_taken2"), sem("xm_hi_step"), sem("xm_split2")
        up_done, up_taken, h_hi_step, h_split, down_done = sem("up_done"), sem("up_taken"), sem("h_hi_step"), sem("h_split"), sem("down_done")
        w1_hi_ready, w1_split, w2_hi_ready, w2_split = sem("w1_hi_ready"), sem("w1_split"), sem("w2_hi_ready"), sem("w2_split")
        acc_taken, acc_step, out_ready = sem("acc_taken"), sem("acc_step"), sem("out_ready")

        x_blocks = x.rearrange("b (n t p) d -> (b n) p t d", t=TT, p=P)
        out_blocks = out.rearrange("b (n t p) d -> (b n) t p d", t=TT, p=P)
        block = ctx.enter_context(nc.Block())

        def gate(b, which):
            return sh.gates[:, bass.ds(b, 1), which, :].rearrange("p a n -> p (a n)")

        @block.sync
        def _(sp):
            def load_y(k):
                group, tok = sp.snap(k // BPB * G), sp.snap(k % BPB * TOK)
                for g in range(G):
                    sp.dma_start(yb[:, g, :], sh.y_cols[bass.ds(group + g, 1), :, bass.ds(tok, TOK)].rearrange("a p n -> p (a n)")).then_inc(y_in[g], 16)

            for c in range(4):
                sp.dma_start(w2_raw[:, c * MT // 4:(c + 1) * MT // 4, :],
                             W2[c * MLP // 4:(c + 1) * MLP // 4, :].rearrange("(j p) n -> p j n", p=P)).then_inc(w2_in[c], 16)
            sp.dma_start(xb[1][:, :, :], x_blocks[1]).then_inc(x_in[1], 16)
            sp.wait_ge(y_split, KT)
            load_y(1)

            def body(k, i, q, load_next):
                if load_next:
                    sp.wait_ge(y_split, KT * (k + 2))
                    load_y(k + 2)
                for t in range(TT):
                    sp.wait_ge(out_ready, TT * k + t + 1)
                    sp.dma_start(out_blocks[k, t], xb[q][:, t, :]).then_inc(stored[q], 16)
                if load_next:
                    sp.wait_ge(stored[q], 16 * TT * (i + 1))
                    sp.dma_start(xb[q][:, :, :], x_blocks[k + 2]).then_inc(x_in[q], 16)

            with sp.Fori(0, NBLK // 2 - 1) as i:
                for q in range(2):
                    body(2 * i + q, i, q, True)
            for q in range(2):
                body(NBLK - 2 + q, NBLK // 2 - 1, q, False)
            for q in range(2):
                sp.wait_ge(stored[q], 16 * TT * NBLK // 2)

        @block.gpsimd
        def _(pool):
            for s, n in ((wo_done, 1), (wo_taken, 1), (t_taken, 1), (xm_split, 4), (up_done, 2), (up_taken, 2),
                         (h_split, 2), (down_done, 2), (acc_taken, 4)):
                pool.sem_inc(s, n)
            for s in (x_in[0], *y_in):
                pool.sem_inc(s, 16)
            pool.memset(neg_half[:, :], -0.5).then_inc(half_ready, 1)
            pool.wait_ge(half_ready, 1)

            def bias_x(i, q, b, t):
                if t == 0:
                    pool.wait_ge(x_in[q], 16 * (i + 1))
                pool.tensor_tensor(xb[q][:, t, :], xb[q][:, t, :], gate(b, GBO), ALU.add).then_inc(x_biased, 1)

            def root(k):
                pool.wait_ge(stats_ready, k + 1)
                pool.tensor_tensor(rstd[:, :], var_eps[:, :], neg_half[:, :], ALU.pow).then_inc(rstd_ready, 1)

            def bias_x1(k, q, b, t):
                if t == 0:
                    pool.wait_ge(xn_ready, k + 1)
                pool.tensor_tensor(xb[q][:, t, :], xb[q][:, t, :], gate(b, GB2), ALU.add).then_inc(x1_biased, 1)

            def split_w1(n, j):
                pool.wait_ge(w1_hi_ready, n + 1)
                pool.tensor_tensor(w1_lo[:, j % 2, :, :], w1_raw[j * 4 // MT][:, :, j % (MT // 4) * P:(j % (MT // 4) + 1) * P], w1_hi[:, j % 2, :, :].bitcast(F32),
                                   ALU.subtract).then_inc(w1_split, 1)

            def split_w2(n, j):
                pool.wait_ge(w2_hi_ready, n + 1)
                pool.tensor_tensor(w2_lo[:, j % 2, :], w2_raw[:, j, :], w2_hi[:, j % 2, :].bitcast(F32), ALU.subtract).then_inc(w2_split, 1)

            def body(k, i, q, b, has_next):
                for j in range(MT):
                    n = MT * k + j
                    if has_next or j < MT - 2:
                        split_w1(n + 2, (j + 2) % MT)
                    if has_next or j < MT - 1:
                        split_w2(n + 1, (j + 1) % MT)
                    if has_next:
                        if 2 <= j < 2 + TT:
                            bias_x(i, 1 - q, b, j - 2)
                        if j == 8:
                            root(k + 1)
                        if 9 <= j < 9 + TT:
                            bias_x1(k + 1, 1 - q, b, j - 9)

            pool.wait_ge(wo_hi_ready, 1)
            pool.tensor_tensor(wo_lo[:, :, :], xn[:, :, :], wo_hi[:, :, :].bitcast(F32), ALU.subtract).then_inc(wo_split, 1)
            for t in range(TT):
                bias_x(0, 0, 0, t)
            root(0)
            split_w1(0, 0)
            split_w1(1, 1)
            split_w2(0, 0)
            for t in range(TT):
                bias_x1(0, 0, 0, t)
            with pool.Fori(0, NBLK // 2 - 1) as i:
                for q in range(2):
                    body(2 * i + q, i + q, q, (2 * i + q + 1) // BPB, True)
            body(NBLK - 2, NBLK // 2 - 1, 0, B - 1, True)
            body(NBLK - 1, 0, 1, B - 1, False)

        @block.vector
        def _(v):
            def split_y(k, gs=range(G)):
                v.wait_ge(wo_done, TT * k + 1)
                for g in gs:
                    v.wait_ge(y_biased, G * k + g + 1)
                    v.tensor_copy(y_hi[:, g, :], yb[:, g, :]).then_inc(y_hi_step, 1)
                    v.wait_ge(y_hi_step, G * k + g + 1)
                    v.tensor_tensor(y_lo[:, g, :], yb[:, g, :], y_hi[:, g, :].bitcast(F32), ALU.subtract).then_inc(y_split, 1)

            def residual(k, q, b, t, bank=o_bank):
                n = TT * k + t
                v.wait_ge(wo_done, 1 + n + 1)
                v.tensor_tensor(gated[:, t, :], bank[:, :], gate(b, G_MSA), ALU.mult).then_inc(wo_taken, 1)
                v.wait_ge(wo_taken, 1 + n + 1)
                v.wait_ge(x_biased, n + 1)
                v.tensor_tensor(xb[q][:, t, :], xb[q][:, t, :], gated[:, t, :], ALU.add).then_inc(x1_step, 1)
                v.wait_ge(x1_step, n + 1)
                v.bn_stats(stats[:, t, :], xb[q][:, t, :]).then_inc(norm_step, 1)

            def variance(k):
                v.wait_ge(norm_step, (TT + 1) * k + TT)
                v.sem_inc(stats_seen, 1)
                for t in range(TT):
                    last = v.bn_aggr(mv[:, t, :], stats[:, t, :])
                last.then_inc(norm_step, 1)
                v.wait_ge(norm_step, (TT + 1) * (k + 1))
                v.tensor_scalar(var_eps[:, :], mv[:, :, 1], EPS, None, ALU.add).then_inc(stats_ready, 1)

            def normalise(k, q):
                v.wait_ge(rstd_ready, k + 1)
                for t in range(TT):
                    last = v.tensor_scalar(xn[:, t, :], xb[q][:, t, :], mv[:, t, 0:1], rstd[:, t:t + 1], ALU.subtract, ALU.mult)
                last.then_inc(xn_ready, 1)

            def split_xm(k):
                v.wait_ge(up_done, MT * k + 2)
                for t in range(KT):
                    v.wait_ge(t_taken, 1 + KT * k + t + 1)
                    v.tensor_copy(xm_hi[:, t, :], xm[:, t, :]).then_inc(xm_hi_step, 1)
                    v.wait_ge(xm_hi_step, KT * k + t + 1)
                    v.tensor_tensor(xm_lo[:, t, :], xm[:, t, :], xm_hi[:, t, :].bitcast(F32), ALU.subtract).then_inc(xm_split, 1)

            def high_w1(n, j):
                v.wait_ge(up_done, n + 1)
                v.tensor_copy(w1_hi[:, j % 2, :, :], w1_raw[j * 4 // MT][:, :, j % (MT // 4) * P:(j % (MT // 4) + 1) * P]).then_inc(w1_hi_ready, 1)

            def high_w2(n, j):
                v.wait_ge(w2_in[j * 4 // MT], 16)
                v.wait_ge(down_done, n + 1)
                v.tensor_copy(w2_hi[:, j % 2, :], w2_raw[:, j, :]).then_inc(w2_hi_ready, 1)

            def split_h(n, j):
                v.wait_ge(up_taken, 2 + n + 1)
                v.wait_ge(down_done, n + 1)
                v.tensor_copy(h_hi[:, j % 2, :], h[:, j % 2, :]).then_inc(h_hi_step, 1)
                v.wait_ge(h_hi_step, n + 1)
                v.tensor_tensor(h_lo[:, j % 2, :], h[:, j % 2, :], h_hi[:, j % 2, :].bitcast(F32), ALU.subtract).then_inc(h_split, 1)

            def result_gated(k, b):
                v.wait_ge(down_done, 2 + MT * (k + 1))
                for t in range(TT):
                    v.tensor_tensor(gated[:, t, :], acc_bank[t][:, :], gate(b, G_MLP), ALU.mult).then_inc(acc_taken, 1)

            def result(k, q):
                v.wait_ge(x1_biased, TT * (k + 1))
                v.wait_ge(acc_taken, 4 + TT * (k + 1))
                for t in range(TT):
                    v.tensor_tensor(xb[q][:, t, :], xb[q][:, t, :], gated[:, t, :], ALU.add).then_inc(out_ready, 1)

            def parts_for(k, j, more_w1=True, more_w2=True):
                n = MT * k + j
                split_h(n, j)
                if more_w1:
                    high_w1(n + 2, (j + 2) % MT)
                if more_w2:
                    high_w2(n + 1, (j + 1) % MT)

            def body(k, q, b, next_b, has_next):
                for j in range(1, MT):
                    parts_for(k, j, has_next or j < MT - 2, has_next or j < MT - 1)
                    if has_next:
                        if j in (1, 2):
                            split_y(k + 1, range((j - 1) * G // 2, j * G // 2))
                        if 3 <= j < 3 + TT:
                            residual(k + 1, 1 - q, next_b, j - 3)
                        if j == 7:
                            variance(k + 1)
                        if j == 8:
                            normalise(k + 1, 1 - q)
                if has_next:
                    split_xm(k + 1)
                result_gated(k, b)
                if has_next:
                    parts_for(k + 1, 0)
                result(k, q)

            v.tensor_copy(wo_hi[:, :, :], xn[:, :, :]).then_inc(wo_hi_ready, 1)
            split_y(0)
            for t in range(TT):
                residual(0, 0, 0, t, first_o[t])
            variance(0)
            v.wait_ge(wo_split, 1)
            normalise(0, 0)
            high_w1(0, 0)
            high_w1(1, 1)
            high_w2(0, 0)
            split_xm(0)
            parts_for(0, 0)
            with v.Fori(0, NBLK // 2 - 1) as i:
                for q in range(2):
                    k = 2 * i + q
                    body(k, q, k // BPB, (k + 1) // BPB, True)
            body(NBLK - 2, 0, B - 1, B - 1, True)
            body(NBLK - 1, 1, B - 1, B - 1, False)

        @block.scalar
        def _(act):
            def bias_y(k):
                for g in range(G):
                    act.wait_ge(y_in[g], 16 * (k + 1))
                    act.activation(yb[:, g, :], yb[:, g, :], ACT.Identity, bias=sh.vecs[:, ROW_BV + g:ROW_BV + g + 1]).then_inc(y_biased, 1)

            def modulate(k, b, t, bank=t_bank):
                act.wait_ge(t_done, KT * k + t + 1)
                act.wait_ge(xm_split, KT * k + t + 1)
                act.activation(xm[:, t, :], bank[:, :], ACT.Identity,
                               scale=sh.mod[:, bass.ds(b, 1), SCALE_MLP + t].rearrange("p a -> p (a)"),
                               bias=sh.mod[:, bass.ds(b, 1), SHIFT_MLP + t].rearrange("p a -> p (a)")).then_inc(t_taken, 1)

            def gelu(n, j):
                act.wait_ge(up_done, 2 + n + 1)
                act.wait_ge(h_split, n + 1)
                act.activation(h[:, j % 2, :], up_bank[j % 2][:, :], ACT.Gelu, bias=sh.vecs[:, ROW_B1 + j:ROW_B1 + j + 1]).then_inc(up_taken, 1)

            def body(k, next_b, has_next):
                for j in range(MT):
                    gelu(MT * k + j, j)
                    if has_next and j == 0:
                        bias_y(k + 1)
                    if has_next and 10 <= j < 10 + KT:
                        modulate(k + 1, next_b, j - 10)

            bias_y(0)
            for t in range(KT):
                modulate(0, 0, t, first_t[t])
            with act.Fori(0, NBLK // 2 - 1) as i:
                for q in range(2):
                    body(2 * i + q, (2 * i + q + 1) // BPB, True)
            body(NBLK - 2, B - 1, True)
            body(NBLK - 1, 0, False)

        @block.tensor
        def _(pe):
            def three(bank, first, last, hi_l, lo_l, hi_r, lo_r):
                pe.matmul(bank, hi_l, hi_r, start=first, stop=False)
                pe.matmul(bank, hi_l, lo_r, start=False, stop=False)
                return pe.matmul(bank, lo_l, hi_r, start=False, stop=last)

            def project_out(k, t, bank=None):
                if bank is None:
                    bank = o_bank
                    pe.wait_ge(wo_taken, TT * k + t + 1)
                s = slice(t * P, (t + 1) * P)
                for g in range(G):
                    if t == 0:
                        pe.wait_ge(y_split, G * k + g + 1)
                    last = three(bank[:, :], g == 0, g == G - 1, y_hi[:, g, s], y_lo[:, g, s], wo_hi[:, g, :], wo_lo[:, g, :])
                last.then_inc(wo_done, 1)

            def transposes(k, t, bank=None):
                if t == 0:
                    pe.wait_ge(xn_ready, k + 1)
                if bank is None:
                    bank = t_bank
                    pe.wait_ge(t_taken, KT * k + t + 1)
                for s in range(TT):
                    last = pe.transpose(bank[:, s * P:(s + 1) * P], xn[:, s, t * P:(t + 1) * P], sh.ident[:, :])
                last.then_inc(t_done, 1)

            def up(k, j):
                n = MT * k + j
                pe.wait_ge(w1_split, n + 1)
                pe.wait_ge(up_taken, n + 1)
                for t in range(KT):
                    if j == 0:
                        pe.wait_ge(xm_split, 4 + KT * k + t + 1)
                    last = three(up_bank[j % 2][:, :], t == 0, t == KT - 1, w1_hi[:, j % 2, t, :], w1_lo[:, j % 2, t, :],
                                 xm_hi[:, t, :], xm_lo[:, t, :])
                last.then_inc(up_done, 1)

            def down(k, j):
                n = MT * k + j
                pe.wait_ge(w2_split, n + 1)
                pe.wait_ge(h_split, 2 + n + 1)
                for t in range(TT):
                    if j == 0:
                        pe.wait_ge(acc_taken, TT * k + t + 1)
                    s = slice(t * P, (t + 1) * P)
                    last = three(acc_bank[t][:, :], j == 0, j == MT - 1, h_hi[:, j % 2, s], h_lo[:, j % 2, s],
                                 w2_hi[:, j % 2, :], w2_lo[:, j % 2, :])
                last.then_inc(down_done, 1)

            def body(k, has_next):
                for j in range(MT):
                    up(k, j)
                    if j:
                        down(k, j - 1)
                    if has_next and 3 <= j < 3 + TT:
                        project_out(k + 1, j - 3)
                    if has_next and 10 <= j < 10 + KT:
                        transposes(k + 1, j - 10)
                down(k, MT - 1)

            pe.wait_ge(wo_split, 1)
            for t in range(TT):
                project_out(0, t, first_o[t])
            for t in range(KT):
                transposes(0, t, first_t[t])
            with pe.Fori(0, NBLK // 2 - 1) as i:
                for q in range(2):
                    body(2 * i + q, True)
            body(NBLK - 2, True)
            body(NBLK - 1, False)


def program(nc, x, cond, Wc, bc, Wq, bq, Wk, bk, Wv, bv, Wo, bo, W1, b1, W2, b2, out):
    with ExitStack() as ctx:
        sh = Shared(nc, ctx)
        project(nc, sh, x, cond, Wc, bc, Wq, bq, Wk, bk, Wv, bv, b1, bo, b2)
        late = Late(nc, ctx)
        attend(nc, sh, late, x, Wo, W1)
        feed_forward(nc, sh, late, x, W2, out)


_INS = ["x", "cond_1024"] + ["L0_cond_" + n for n in "Wc bc Wq bq Wk bk Wv bv Wo bo W1 b1 W2 b2".split()]


def kernel(**inputs):
    import numpy as np
    import concourse.bacc as bacc
    from concourse.bass_utils import run_bass_kernel_spmd

    nc = bacc.Bacc("TRN2", target_bir_lowering=False, num_devices=1)
    arrays, args = {}, []
    for name in _INS:
        a = np.ascontiguousarray(inputs[name])
        arrays[f"in_{name}"] = a
        args.append(nc.dram_tensor(f"in_{name}", a.shape, mybir.dt.from_np(a.dtype), kind="ExternalInput").ap())
    out = nc.dram_tensor("out", (B, S, H), F32, kind="ExternalOutput").ap()
    program(nc, *args, out)
    r = run_bass_kernel_spmd(nc, [arrays], core_ids=[0])
    return r.results[0]["out"]
```
